# Optimizing a Trainium2 kernel written in Bass

```python
import numpy as np
import jax
import jax.numpy as jnp

def _softmax(x, axis=-1):
    return jax.nn.softmax(x, axis=axis)

def _gelu(x):
    return jax.nn.gelu(x, approximate=True)

def _silu(x):
    return jax.nn.silu(x)

def _sigmoid(x):
    return jax.nn.sigmoid(x)

def _layernorm(x, axis=-1, eps=1e-05):
    m = jnp.mean(x, axis=axis, keepdims=True)
    v = jnp.var(x, axis=axis, keepdims=True)
    return (x - m) / jnp.sqrt(v + eps)

def _scatter_add(tgt, idx, src, axis=0):
    return tgt.at[idx].add(src)

def _segment_sum(src, seg, n):
    return jax.ops.segment_sum(src, seg, n)
kernel_name = 'mk_rec_standalone_d1_rec_r8_ed65d7'

def setup_inputs(seed: int=0):
    np.random.seed(seed)
    _w = jnp.asarray

    def _rec_inputs():
        import jax
        import jax.numpy as jnp
        _rk = jax.random.key(seed)
        r_user_id = jax.random.randint(jax.random.fold_in(_rk, 1), (2048,), 72, 99964, jnp.int32)
        r_target_tag = jax.random.randint(jax.random.fold_in(_rk, 2), (2048,), 67, 99986, jnp.int32)
        r_target_artist = jax.random.randint(jax.random.fold_in(_rk, 3), (2048,), 18, 99955, jnp.int32)
        r_hist_tags = jnp.stack([jax.random.randint(jax.random.fold_in(jax.random.fold_in(_rk, 4), 0), (2048,), 6, 99964, jnp.int32), jax.random.randint(jax.random.fold_in(jax.random.fold_in(_rk, 4), 1), (2048,), 2, 99994, jnp.int32), jax.random.randint(jax.random.fold_in(jax.random.fold_in(_rk, 4), 2), (2048,), 29, 99990, jnp.int32), jax.random.randint(jax.random.fold_in(jax.random.fold_in(_rk, 4), 3), (2048,), 8, 99923, jnp.int32), jax.random.randint(jax.random.fold_in(jax.random.fold_in(_rk, 4), 4), (2048,), 17, 99972, jnp.int32), jax.random.randint(jax.random.fold_in(jax.random.fold_in(_rk, 4), 5), (2048,), 5, 99959, jnp.int32), jax.random.randint(jax.random.fold_in(jax.random.fold_in(_rk, 4), 6), (2048,), 18, 99989, jnp.int32), jax.random.randint(jax.random.fold_in(jax.random.fold_in(_rk, 4), 7), (2048,), 5, 99966, jnp.int32), jax.random.randint(jax.random.fold_in(jax.random.fold_in(_rk, 4), 8), (2048,), 9, 99966, jnp.int32), jax.random.randint(jax.random.fold_in(jax.random.fold_in(_rk, 4), 9), (2048,), 46, 99989, jnp.int32), jax.random.randint(jax.random.fold_in(jax.random.fold_in(_rk, 4), 10), (2048,), 1, 99994, jnp.int32), jax.random.randint(jax.random.fold_in(jax.random.fold_in(_rk, 4), 11), (2048,), 1, 12499, jnp.int32), jax.random.randint(jax.random.fold_in(jax.random.fold_in(_rk, 4), 12), (2048,), 15, 99989, jnp.int32), jax.random.randint(jax.random.fold_in(jax.random.fold_in(_rk, 4), 13), (2048,), 13, 99990, jnp.int32), jax.random.randint(jax.random.fold_in(jax.random.fold_in(_rk, 4), 14), (2048,), 62, 99963, jnp.int32), jax.random.randint(jax.random.fold_in(jax.random.fold_in(_rk, 4), 15), (2048,), 6, 99980, jnp.int32), jax.random.randint(jax.random.fold_in(jax.random.fold_in(_rk, 4), 16), (2048,), 0, 99996, jnp.int32), jax.random.randint(jax.random.fold_in(jax.random.fold_in(_rk, 4), 17), (2048,), 11, 99990, jnp.int32), jax.random.randint(jax.random.fold_in(jax.random.fold_in(_rk, 4), 18), (2048,), 13, 99996, jnp.int32), jax.random.randint(jax.random.fold_in(jax.random.fold_in(_rk, 4), 19), (2048,), 81, 99983, jnp.int32), jax.random.randint(jax.random.fold_in(jax.random.fold_in(_rk, 4), 20), (2048,), 25, 12497, jnp.int32), jax.random.randint(jax.random.fold_in(jax.random.fold_in(_rk, 4), 21), (2048,), 77, 99998, jnp.int32), jax.random.randint(jax.random.fold_in(jax.random.fold_in(_rk, 4), 22), (2048,), 15, 99978, jnp.int32), jax.random.randint(jax.random.fold_in(jax.random.fold_in(_rk, 4), 23), (2048,), 25, 99998, jnp.int32), jax.random.randint(jax.random.fold_in(jax.random.fold_in(_rk, 4), 24), (2048,), 15, 99987, jnp.int32), jax.random.randint(jax.random.fold_in(jax.random.fold_in(_rk, 4), 25), (2048,), 20, 99970, jnp.int32), jax.random.randint(jax.random.fold_in(jax.random.fold_in(_rk, 4), 26), (2048,), 6, 99967, jnp.int32), jax.random.randint(jax.random.fold_in(jax.random.fold_in(_rk, 4), 27), (2048,), 9, 12499, jnp.int32), jax.random.randint(jax.random.fold_in(jax.random.fold_in(_rk, 4), 28), (2048,), 75, 99967, jnp.int32), jax.random.randint(jax.random.fold_in(jax.random.fold_in(_rk, 4), 29), (2048,), 22, 99974, jnp.int32), jax.random.randint(jax.random.fold_in(jax.random.fold_in(_rk, 4), 30), (2048,), 13, 99982, jnp.int32), jax.random.randint(jax.random.fold_in(jax.random.fold_in(_rk, 4), 31), (2048,), 10, 99954, jnp.int32), jax.random.randint(jax.random.fold_in(jax.random.fold_in(_rk, 4), 32), (2048,), 12, 99932, jnp.int32), jax.random.randint(jax.random.fold_in(jax.random.fold_in(_rk, 4), 33), (2048,), 10, 99996, jnp.int32), jax.random.randint(jax.random.fold_in(jax.random.fold_in(_rk, 4), 34), (2048,), 10, 99946, jnp.int32), jax.random.randint(jax.random.fold_in(jax.random.fold_in(_rk, 4), 35), (2048,), 0, 99999, jnp.int32), jax.random.randint(jax.random.fold_in(jax.random.fold_in(_rk, 4), 36), (2048,), 54, 99958, jnp.int32), jax.random.randint(jax.random.fold_in(jax.random.fold_in(_rk, 4), 37), (2048,), 59, 99999, jnp.int32), jax.random.randint(jax.random.fold_in(jax.random.fold_in(_rk, 4), 38), (2048,), 0, 12499, jnp.int32), jax.random.randint(jax.random.fold_in(jax.random.fold_in(_rk, 4), 39), (2048,), 42, 99983, jnp.int32), jax.random.randint(jax.random.fold_in(jax.random.fold_in(_rk, 4), 40), (2048,), 40, 99989, jnp.int32), jax.random.randint(jax.random.fold_in(jax.random.fold_in(_rk, 4), 41), (2048,), 62, 99975, jnp.int32), jax.random.randint(jax.random.fold_in(jax.random.fold_in(_rk, 4), 42), (2048,), 17, 99982, jnp.int32), jax.random.randint(jax.random.fold_in(jax.random.fold_in(_rk, 4), 43), (2048,), 22, 99988, jnp.int32), jax.random.randint(jax.random.fold_in(jax.random.fold_in(_rk, 4), 44), (2048,), 5, 99967, jnp.int32), jax.random.randint(jax.random.fold_in(jax.random.fold_in(_rk, 4), 45), (2048,), 36, 99994, jnp.int32), jax.random.randint(jax.random.fold_in(jax.random.fold_in(_rk, 4), 46), (2048,), 0, 99970, jnp.int32), jax.random.randint(jax.random.fold_in(jax.random.fold_in(_rk, 4), 47), (2048,), 88, 99964, jnp.int32), jax.random.randint(jax.random.fold_in(jax.random.fold_in(_rk, 4), 48), (2048,), 16, 99931, jnp.int32), jax.random.randint(jax.random.fold_in(jax.random.fold_in(_rk, 4), 49), (2048,), 24, 99991, jnp.int32), jax.random.randint(jax.random.fold_in(jax.random.fold_in(_rk, 4), 50), (2048,), 26, 99946, jnp.int32), jax.random.randint(jax.random.fold_in(jax.random.fold_in(_rk, 4), 51), (2048,), 13, 12499, jnp.int32), jax.random.randint(jax.random.fold_in(jax.random.fold_in(_rk, 4), 52), (2048,), 33, 99981, jnp.int32), jax.random.randint(jax.random.fold_in(jax.random.fold_in(_rk, 4), 53), (2048,), 11, 12490, jnp.int32), jax.random.randint(jax.random.fold_in(jax.random.fold_in(_rk, 4), 54), (2048,), 55, 99981, jnp.int32), jax.random.randint(jax.random.fold_in(jax.random.fold_in(_rk, 4), 55), (2048,), 34, 99953, jnp.int32), jax.random.randint(jax.random.fold_in(jax.random.fold_in(_rk, 4), 56), (2048,), 41, 12496, jnp.int32), jax.random.randint(jax.random.fold_in(jax.random.fold_in(_rk, 4), 57), (2048,), 3, 12499, jnp.int32), jax.random.randint(jax.random.fold_in(jax.random.fold_in(_rk, 4), 58), (2048,), 24, 99996, jnp.int32), jax.random.randint(jax.random.fold_in(jax.random.fold_in(_rk, 4), 59), (2048,), 19, 99981, jnp.int32), jax.random.randint(jax.random.fold_in(jax.random.fold_in(_rk, 4), 60), (2048,), 4, 99959, jnp.int32), jax.random.randint(jax.random.fold_in(jax.random.fold_in(_rk, 4), 61), (2048,), 2, 99974, jnp.int32), jax.random.randint(jax.random.fold_in(jax.random.fold_in(_rk, 4), 62), (2048,), 70, 99972, jnp.int32), jax.random.randint(jax.random.fold_in(jax.random.fold_in(_rk, 4), 63), (2048,), 9, 99941, jnp.int32), jax.random.randint(jax.random.fold_in(jax.random.fold_in(_rk, 4), 64), (2048,), 5, 99942, jnp.int32), jax.random.randint(jax.random.fold_in(jax.random.fold_in(_rk, 4), 65), (2048,), 11, 99938, jnp.int32), jax.random.randint(jax.random.fold_in(jax.random.fold_in(_rk, 4), 66), (2048,), 2, 99978, jnp.int32), jax.random.randint(jax.random.fold_in(jax.random.fold_in(_rk, 4), 67), (2048,), 36, 99935, jnp.int32), jax.random.randint(jax.random.fold_in(jax.random.fold_in(_rk, 4), 68), (2048,), 11, 99990, jnp.int32), jax.random.randint(jax.random.fold_in(jax.random.fold_in(_rk, 4), 69), (2048,), 18, 99985, jnp.int32), jax.random.randint(jax.random.fold_in(jax.random.fold_in(_rk, 4), 70), (2048,), 25, 12498, jnp.int32), jax.random.randint(jax.random.fold_in(jax.random.fold_in(_rk, 4), 71), (2048,), 83, 99925, jnp.int32), jax.random.randint(jax.random.fold_in(jax.random.fold_in(_rk, 4), 72), (2048,), 35, 99958, jnp.int32), jax.random.randint(jax.random.fold_in(jax.random.fold_in(_rk, 4), 73), (2048,), 62, 99975, jnp.int32), jax.random.randint(jax.random.fold_in(jax.random.fold_in(_rk, 4), 74), (2048,), 3, 99994, jnp.int32), jax.random.randint(jax.random.fold_in(jax.random.fold_in(_rk, 4), 75), (2048,), 10, 99981, jnp.int32), jax.random.randint(jax.random.fold_in(jax.random.fold_in(_rk, 4), 76), (2048,), 22, 99987, jnp.int32), jax.random.randint(jax.random.fold_in(jax.random.fold_in(_rk, 4), 77), (2048,), 36, 99972, jnp.int32), jax.random.randint(jax.random.fold_in(jax.random.fold_in(_rk, 4), 78), (2048,), 3, 99991, jnp.int32), jax.random.randint(jax.random.fold_in(jax.random.fold_in(_rk, 4), 79), (2048,), 59, 99977, jnp.int32), jax.random.randint(jax.random.fold_in(jax.random.fold_in(_rk, 4), 80), (2048,), 16, 99945, jnp.int32), jax.random.randint(jax.random.fold_in(jax.random.fold_in(_rk, 4), 81), (2048,), 48, 12500, jnp.int32), jax.random.randint(jax.random.fold_in(jax.random.fold_in(_rk, 4), 82), (2048,), 6, 99946, jnp.int32), jax.random.randint(jax.random.fold_in(jax.random.fold_in(_rk, 4), 83), (2048,), 85, 12497, jnp.int32), jax.random.randint(jax.random.fold_in(jax.random.fold_in(_rk, 4), 84), (2048,), 0, 99989, jnp.int32), jax.random.randint(jax.random.fold_in(jax.random.fold_in(_rk, 4), 85), (2048,), 26, 12498, jnp.int32), jax.random.randint(jax.random.fold_in(jax.random.fold_in(_rk, 4), 86), (2048,), 1, 99996, jnp.int32), jax.random.randint(jax.random.fold_in(jax.random.fold_in(_rk, 4), 87), (2048,), 70, 99996, jnp.int32), jax.random.randint(jax.random.fold_in(jax.random.fold_in(_rk, 4), 88), (2048,), 3, 99999, jnp.int32), jax.random.randint(jax.random.fold_in(jax.random.fold_in(_rk, 4), 89), (2048,), 6, 99950, jnp.int32), jax.random.randint(jax.random.fold_in(jax.random.fold_in(_rk, 4), 90), (2048,), 5, 99999, jnp.int32), jax.random.randint(jax.random.fold_in(jax.random.fold_in(_rk, 4), 91), (2048,), 10, 99957, jnp.int32), jax.random.randint(jax.random.fold_in(jax.random.fold_in(_rk, 4), 92), (2048,), 10, 99931, jnp.int32), jax.random.randint(jax.random.fold_in(jax.random.fold_in(_rk, 4), 93), (2048,), 6, 99990, jnp.int32), jax.random.randint(jax.random.fold_in(jax.random.fold_in(_rk, 4), 94), (2048,), 7, 99988, jnp.int32), jax.random.randint(jax.random.fold_in(jax.random.fold_in(_rk, 4), 95), (2048,), 46, 99996, jnp.int32), jax.random.randint(jax.random.fold_in(jax.random.fold_in(_rk, 4), 96), (2048,), 48, 12490, jnp.int32), jax.random.randint(jax.random.fold_in(jax.random.fold_in(_rk, 4), 97), (2048,), 4, 99997, jnp.int32), jax.random.randint(jax.random.fold_in(jax.random.fold_in(_rk, 4), 98), (2048,), 0, 99943, jnp.int32), jax.random.randint(jax.random.fold_in(jax.random.fold_in(_rk, 4), 99), (2048,), 28, 99985, jnp.int32), jax.random.randint(jax.random.fold_in(jax.random.fold_in(_rk, 4), 100), (2048,), 6, 99983, jnp.int32), jax.random.randint(jax.random.fold_in(jax.random.fold_in(_rk, 4), 101), (2048,), 4, 99962, jnp.int32), jax.random.randint(jax.random.fold_in(jax.random.fold_in(_rk, 4), 102), (2048,), 130, 12491, jnp.int32), jax.random.randint(jax.random.fold_in(jax.random.fold_in(_rk, 4), 103), (2048,), 8, 99996, jnp.int32), jax.random.randint(jax.random.fold_in(jax.random.fold_in(_rk, 4), 104), (2048,), 2, 99958, jnp.int32), jax.random.randint(jax.random.fold_in(jax.random.fold_in(_rk, 4), 105), (2048,), 9, 99982, jnp.int32), jax.random.randint(jax.random.fold_in(jax.random.fold_in(_rk, 4), 106), (2048,), 15, 99995, jnp.int32), jax.random.randint(jax.random.fold_in(jax.random.fold_in(_rk, 4), 107), (2048,), 8, 99997, jnp.int32), jax.random.randint(jax.random.fold_in(jax.random.fold_in(_rk, 4), 108), (2048,), 45, 99979, jnp.int32), jax.random.randint(jax.random.fold_in(jax.random.fold_in(_rk, 4), 109), (2048,), 12, 99989, jnp.int32), jax.random.randint(jax.random.fold_in(jax.random.fold_in(_rk, 4), 110), (2048,), 9, 99948, jnp.int32), jax.random.randint(jax.random.fold_in(jax.random.fold_in(_rk, 4), 111), (2048,), 23, 99975, jnp.int32), jax.random.randint(jax.random.fold_in(jax.random.fold_in(_rk, 4), 112), (2048,), 30, 99994, jnp.int32), jax.random.randint(jax.random.fold_in(jax.random.fold_in(_rk, 4), 113), (2048,), 3, 99985, jnp.int32), jax.random.randint(jax.random.fold_in(jax.random.fold_in(_rk, 4), 114), (2048,), 37, 12498, jnp.int32), jax.random.randint(jax.random.fold_in(jax.random.fold_in(_rk, 4), 115), (2048,), 39, 99982, jnp.int32), jax.random.randint(jax.random.fold_in(jax.random.fold_in(_rk, 4), 116), (2048,), 1, 12497, jnp.int32), jax.random.randint(jax.random.fold_in(jax.random.fold_in(_rk, 4), 117), (2048,), 0, 99998, jnp.int32), jax.random.randint(jax.random.fold_in(jax.random.fold_in(_rk, 4), 118), (2048,), 31, 12498, jnp.int32), jax.random.randint(jax.random.fold_in(jax.random.fold_in(_rk, 4), 119), (2048,), 0, 12494, jnp.int32), jax.random.randint(jax.random.fold_in(jax.random.fold_in(_rk, 4), 120), (2048,), 24, 99982, jnp.int32), jax.random.randint(jax.random.fold_in(jax.random.fold_in(_rk, 4), 121), (2048,), 3, 99942, jnp.int32), jax.random.randint(jax.random.fold_in(jax.random.fold_in(_rk, 4), 122), (2048,), 85, 99980, jnp.int32), jax.random.randint(jax.random.fold_in(jax.random.fold_in(_rk, 4), 123), (2048,), 39, 99993, jnp.int32), jax.random.randint(jax.random.fold_in(jax.random.fold_in(_rk, 4), 124), (2048,), 22, 99986, jnp.int32), jax.random.randint(jax.random.fold_in(jax.random.fold_in(_rk, 4), 125), (2048,), 74, 99993, jnp.int32), jax.random.randint(jax.random.fold_in(jax.random.fold_in(_rk, 4), 126), (2048,), 4, 12496, jnp.int32), jax.random.randint(jax.random.fold_in(jax.random.fold_in(_rk, 4), 127), (2048,), 35, 99991, jnp.int32), jax.random.randint(jax.random.fold_in(jax.random.fold_in(_rk, 4), 128), (2048,), 0, 99948, jnp.int32), jax.random.randint(jax.random.fold_in(jax.random.fold_in(_rk, 4), 129), (2048,), 7, 99993, jnp.int32), jax.random.randint(jax.random.fold_in(jax.random.fold_in(_rk, 4), 130), (2048,), 27, 12499, jnp.int32), jax.random.randint(jax.random.fold_in(jax.random.fold_in(_rk, 4), 131), (2048,), 6, 99926, jnp.int32), jax.random.randint(jax.random.fold_in(jax.random.fold_in(_rk, 4), 132), (2048,), 29, 99967, jnp.int32), jax.random.randint(jax.random.fold_in(jax.random.fold_in(_rk, 4), 133), (2048,), 54, 12500, jnp.int32), jax.random.randint(jax.random.fold_in(jax.random.fold_in(_rk, 4), 134), (2048,), 17, 99998, jnp.int32), jax.random.randint(jax.random.fold_in(jax.random.fold_in(_rk, 4), 135), (2048,), 4, 99956, jnp.int32), jax.random.randint(jax.random.fold_in(jax.random.fold_in(_rk, 4), 136), (2048,), 146, 99990, jnp.int32), jax.random.randint(jax.random.fold_in(jax.random.fold_in(_rk, 4), 137), (2048,), 4, 99993, jnp.int32), jax.random.randint(jax.random.fold_in(jax.random.fold_in(_rk, 4), 138), (2048,), 5, 12500, jnp.int32), jax.random.randint(jax.random.fold_in(jax.random.fold_in(_rk, 4), 139), (2048,), 1, 99972, jnp.int32), jax.random.randint(jax.random.fold_in(jax.random.fold_in(_rk, 4), 140), (2048,), 30, 99967, jnp.int32), jax.random.randint(jax.random.fold_in(jax.random.fold_in(_rk, 4), 141), (2048,), 19, 99985, jnp.int32), jax.random.randint(jax.random.fold_in(jax.random.fold_in(_rk, 4), 142), (2048,), 75, 99997, jnp.int32), jax.random.randint(jax.random.fold_in(jax.random.fold_in(_rk, 4), 143), (2048,), 16, 99945, jnp.int32), jax.random.randint(jax.random.fold_in(jax.random.fold_in(_rk, 4), 144), (2048,), 35, 99963, jnp.int32), jax.random.randint(jax.random.fold_in(jax.random.fold_in(_rk, 4), 145), (2048,), 8, 99979, jnp.int32), jax.random.randint(jax.random.fold_in(jax.random.fold_in(_rk, 4), 146), (2048,), 21, 99994, jnp.int32), jax.random.randint(jax.random.fold_in(jax.random.fold_in(_rk, 4), 147), (2048,), 9, 99993, jnp.int32), jax.random.randint(jax.random.fold_in(jax.random.fold_in(_rk, 4), 148), (2048,), 1, 99982, jnp.int32), jax.random.randint(jax.random.fold_in(jax.random.fold_in(_rk, 4), 149), (2048,), 1, 99980, jnp.int32), jax.random.randint(jax.random.fold_in(jax.random.fold_in(_rk, 4), 150), (2048,), 5, 99990, jnp.int32), jax.random.randint(jax.random.fold_in(jax.random.fold_in(_rk, 4), 151), (2048,), 26, 99990, jnp.int32), jax.random.randint(jax.random.fold_in(jax.random.fold_in(_rk, 4), 152), (2048,), 0, 99979, jnp.int32), jax.random.randint(jax.random.fold_in(jax.random.fold_in(_rk, 4), 153), (2048,), 53, 99921, jnp.int32), jax.random.randint(jax.random.fold_in(jax.random.fold_in(_rk, 4), 154), (2048,), 0, 99990, jnp.int32), jax.random.randint(jax.random.fold_in(jax.random.fold_in(_rk, 4), 155), (2048,), 1, 99979, jnp.int32), jax.random.randint(jax.random.fold_in(jax.random.fold_in(_rk, 4), 156), (2048,), 10, 99981, jnp.int32), jax.random.randint(jax.random.fold_in(jax.random.fold_in(_rk, 4), 157), (2048,), 11, 99993, jnp.int32), jax.random.randint(jax.random.fold_in(jax.random.fold_in(_rk, 4), 158), (2048,), 22, 99955, jnp.int32), jax.random.randint(jax.random.fold_in(jax.random.fold_in(_rk, 4), 159), (2048,), 4, 99963, jnp.int32), jax.random.randint(jax.random.fold_in(jax.random.fold_in(_rk, 4), 160), (2048,), 8, 99989, jnp.int32), jax.random.randint(jax.random.fold_in(jax.random.fold_in(_rk, 4), 161), (2048,), 77, 99995, jnp.int32), jax.random.randint(jax.random.fold_in(jax.random.fold_in(_rk, 4), 162), (2048,), 9, 99999, jnp.int32), jax.random.randint(jax.random.fold_in(jax.random.fold_in(_rk, 4), 163), (2048,), 27, 99965, jnp.int32), jax.random.randint(jax.random.fold_in(jax.random.fold_in(_rk, 4), 164), (2048,), 1, 99955, jnp.int32), jax.random.randint(jax.random.fold_in(jax.random.fold_in(_rk, 4), 165), (2048,), 46, 12498, jnp.int32), jax.random.randint(jax.random.fold_in(jax.random.fold_in(_rk, 4), 166), (2048,), 1, 99998, jnp.int32), jax.random.randint(jax.random.fold_in(jax.random.fold_in(_rk, 4), 167), (2048,), 35, 99978, jnp.int32), jax.random.randint(jax.random.fold_in(jax.random.fold_in(_rk, 4), 168), (2048,), 0, 99985, jnp.int32), jax.random.randint(jax.random.fold_in(jax.random.fold_in(_rk, 4), 169), (2048,), 62, 99979, jnp.int32), jax.random.randint(jax.random.fold_in(jax.random.fold_in(_rk, 4), 170), (2048,), 49, 99959, jnp.int32), jax.random.randint(jax.random.fold_in(jax.random.fold_in(_rk, 4), 171), (2048,), 4, 99979, jnp.int32), jax.random.randint(jax.random.fold_in(jax.random.fold_in(_rk, 4), 172), (2048,), 86, 99983, jnp.int32), jax.random.randint(jax.random.fold_in(jax.random.fold_in(_rk, 4), 173), (2048,), 2, 99997, jnp.int32), jax.random.randint(jax.random.fold_in(jax.random.fold_in(_rk, 4), 174), (2048,), 24, 12497, jnp.int32), jax.random.randint(jax.random.fold_in(jax.random.fold_in(_rk, 4), 175), (2048,), 44, 99998, jnp.int32), jax.random.randint(jax.random.fold_in(jax.random.fold_in(_rk, 4), 176), (2048,), 39, 99991, jnp.int32), jax.random.randint(jax.random.fold_in(jax.random.fold_in(_rk, 4), 177), (2048,), 2, 99953, jnp.int32), jax.random.randint(jax.random.fold_in(jax.random.fold_in(_rk, 4), 178), (2048,), 0, 12500, jnp.int32), jax.random.randint(jax.random.fold_in(jax.random.fold_in(_rk, 4), 179), (2048,), 55, 99949, jnp.int32), jax.random.randint(jax.random.fold_in(jax.random.fold_in(_rk, 4), 180), (2048,), 16, 12499, jnp.int32), jax.random.randint(jax.random.fold_in(jax.random.fold_in(_rk, 4), 181), (2048,), 8, 99982, jnp.int32), jax.random.randint(jax.random.fold_in(jax.random.fold_in(_rk, 4), 182), (2048,), 40, 99995, jnp.int32), jax.random.randint(jax.random.fold_in(jax.random.fold_in(_rk, 4), 183), (2048,), 13, 99972, jnp.int32), jax.random.randint(jax.random.fold_in(jax.random.fold_in(_rk, 4), 184), (2048,), 15, 99997, jnp.int32), jax.random.randint(jax.random.fold_in(jax.random.fold_in(_rk, 4), 185), (2048,), 24, 99889, jnp.int32), jax.random.randint(jax.random.fold_in(jax.random.fold_in(_rk, 4), 186), (2048,), 18, 99998, jnp.int32), jax.random.randint(jax.random.fold_in(jax.random.fold_in(_rk, 4), 187), (2048,), 13, 99994, jnp.int32), jax.random.randint(jax.random.fold_in(jax.random.fold_in(_rk, 4), 188), (2048,), 0, 12498, jnp.int32), jax.random.randint(jax.random.fold_in(jax.random.fold_in(_rk, 4), 189), (2048,), 46, 99989, jnp.int32), jax.random.randint(jax.random.fold_in(jax.random.fold_in(_rk, 4), 190), (2048,), 40, 99937, jnp.int32), jax.random.randint(jax.random.fold_in(jax.random.fold_in(_rk, 4), 191), (2048,), 20, 12498, jnp.int32), jax.random.randint(jax.random.fold_in(jax.random.fold_in(_rk, 4), 192), (2048,), 0, 99990, jnp.int32), jax.random.randint(jax.random.fold_in(jax.random.fold_in(_rk, 4), 193), (2048,), 30, 99959, jnp.int32), jax.random.randint(jax.random.fold_in(jax.random.fold_in(_rk, 4), 194), (2048,), 30, 99962, jnp.int32), jax.random.randint(jax.random.fold_in(jax.random.fold_in(_rk, 4), 195), (2048,), 34, 99997, jnp.int32), jax.random.randint(jax.random.fold_in(jax.random.fold_in(_rk, 4), 196), (2048,), 23, 99972, jnp.int32), jax.random.randint(jax.random.fold_in(jax.random.fold_in(_rk, 4), 197), (2048,), 46, 99975, jnp.int32), jax.random.randint(jax.random.fold_in(jax.random.fold_in(_rk, 4), 198), (2048,), 25, 99969, jnp.int32), jax.random.randint(jax.random.fold_in(jax.random.fold_in(_rk, 4), 199), (2048,), 2, 99966, jnp.int32)], axis=1)
        r_hist_artists = jnp.stack([jax.random.randint(jax.random.fold_in(jax.random.fold_in(_rk, 5), 0), (2048,), 47, 99967, jnp.int32), jax.random.randint(jax.random.fold_in(jax.random.fold_in(_rk, 5), 1), (2048,), 2, 99982, jnp.int32), jax.random.randint(jax.random.fold_in(jax.random.fold_in(_rk, 5), 2), (2048,), 12, 12496, jnp.int32), jax.random.randint(jax.random.fold_in(jax.random.fold_in(_rk, 5), 3), (2048,), 12, 12492, jnp.int32), jax.random.randint(jax.random.fold_in(jax.random.fold_in(_rk, 5), 4), (2048,), 6, 99980, jnp.int32), jax.random.randint(jax.random.fold_in(jax.random.fold_in(_rk, 5), 5), (2048,), 20, 99988, jnp.int32), jax.random.randint(jax.random.fold_in(jax.random.fold_in(_rk, 5), 6), (2048,), 47, 99999, jnp.int32), jax.random.randint(jax.random.fold_in(jax.random.fold_in(_rk, 5), 7), (2048,), 4, 99974, jnp.int32), jax.random.randint(jax.random.fold_in(jax.random.fold_in(_rk, 5), 8), (2048,), 100, 12495, jnp.int32), jax.random.randint(jax.random.fold_in(jax.random.fold_in(_rk, 5), 9), (2048,), 11, 99998, jnp.int32), jax.random.randint(jax.random.fold_in(jax.random.fold_in(_rk, 5), 10), (2048,), 65, 12500, jnp.int32), jax.random.randint(jax.random.fold_in(jax.random.fold_in(_rk, 5), 11), (2048,), 42, 99979, jnp.int32), jax.random.randint(jax.random.fold_in(jax.random.fold_in(_rk, 5), 12), (2048,), 57, 99974, jnp.int32), jax.random.randint(jax.random.fold_in(jax.random.fold_in(_rk, 5), 13), (2048,), 2, 99978, jnp.int32), jax.random.randint(jax.random.fold_in(jax.random.fold_in(_rk, 5), 14), (2048,), 26, 99925, jnp.int32), jax.random.randint(jax.random.fold_in(jax.random.fold_in(_rk, 5), 15), (2048,), 8, 99999, jnp.int32), jax.random.randint(jax.random.fold_in(jax.random.fold_in(_rk, 5), 16), (2048,), 115, 99979, jnp.int32), jax.random.randint(jax.random.fold_in(jax.random.fold_in(_rk, 5), 17), (2048,), 45, 12500, jnp.int32), jax.random.randint(jax.random.fold_in(jax.random.fold_in(_rk, 5), 18), (2048,), 9, 99954, jnp.int32), jax.random.randint(jax.random.fold_in(jax.random.fold_in(_rk, 5), 19), (2048,), 25, 12497, jnp.int32), jax.random.randint(jax.random.fold_in(jax.random.fold_in(_rk, 5), 20), (2048,), 35, 99899, jnp.int32), jax.random.randint(jax.random.fold_in(jax.random.fold_in(_rk, 5), 21), (2048,), 6, 99999, jnp.int32), jax.random.randint(jax.random.fold_in(jax.random.fold_in(_rk, 5), 22), (2048,), 49, 99994, jnp.int32), jax.random.randint(jax.random.fold_in(jax.random.fold_in(_rk, 5), 23), (2048,), 28, 99983, jnp.int32), jax.random.randint(jax.random.fold_in(jax.random.fold_in(_rk, 5), 24), (2048,), 24, 99987, jnp.int32), jax.random.randint(jax.random.fold_in(jax.random.fold_in(_rk, 5), 25), (2048,), 44, 12497, jnp.int32), jax.random.randint(jax.random.fold_in(jax.random.fold_in(_rk, 5), 26), (2048,), 40, 99972, jnp.int32), jax.random.randint(jax.random.fold_in(jax.random.fold_in(_rk, 5), 27), (2048,), 6, 99981, jnp.int32), jax.random.randint(jax.random.fold_in(jax.random.fold_in(_rk, 5), 28), (2048,), 27, 12498, jnp.int32), jax.random.randint(jax.random.fold_in(jax.random.fold_in(_rk, 5), 29), (2048,), 48, 99978, jnp.int32), jax.random.randint(jax.random.fold_in(jax.random.fold_in(_rk, 5), 30), (2048,), 11, 99983, jnp.int32), jax.random.randint(jax.random.fold_in(jax.random.fold_in(_rk, 5), 31), (2048,), 16, 12493, jnp.int32), jax.random.randint(jax.random.fold_in(jax.random.fold_in(_rk, 5), 32), (2048,), 37, 99981, jnp.int32), jax.random.randint(jax.random.fold_in(jax.random.fold_in(_rk, 5), 33), (2048,), 48, 99979, jnp.int32), jax.random.randint(jax.random.fold_in(jax.random.fold_in(_rk, 5), 34), (2048,), 41, 99988, jnp.int32), jax.random.randint(jax.random.fold_in(jax.random.fold_in(_rk, 5), 35), (2048,), 7, 99987, jnp.int32), jax.random.randint(jax.random.fold_in(jax.random.fold_in(_rk, 5), 36), (2048,), 49, 99963, jnp.int32), jax.random.randint(jax.random.fold_in(jax.random.fold_in(_rk, 5), 37), (2048,), 18, 99985, jnp.int32), jax.random.randint(jax.random.fold_in(jax.random.fold_in(_rk, 5), 38), (2048,), 103, 99956, jnp.int32), jax.random.randint(jax.random.fold_in(jax.random.fold_in(_rk, 5), 39), (2048,), 5, 99995, jnp.int32), jax.random.randint(jax.random.fold_in(jax.random.fold_in(_rk, 5), 40), (2048,), 27, 99953, jnp.int32), jax.random.randint(jax.random.fold_in(jax.random.fold_in(_rk, 5), 41), (2048,), 3, 12498, jnp.int32), jax.random.randint(jax.random.fold_in(jax.random.fold_in(_rk, 5), 42), (2048,), 19, 99964, jnp.int32), jax.random.randint(jax.random.fold_in(jax.random.fold_in(_rk, 5), 43), (2048,), 41, 99986, jnp.int32), jax.random.randint(jax.random.fold_in(jax.random.fold_in(_rk, 5), 44), (2048,), 20, 99998, jnp.int32), jax.random.randint(jax.random.fold_in(jax.random.fold_in(_rk, 5), 45), (2048,), 55, 99943, jnp.int32), jax.random.randint(jax.random.fold_in(jax.random.fold_in(_rk, 5), 46), (2048,), 9, 12500, jnp.int32), jax.random.randint(jax.random.fold_in(jax.random.fold_in(_rk, 5), 47), (2048,), 13, 99972, jnp.int32), jax.random.randint(jax.random.fold_in(jax.random.fold_in(_rk, 5), 48), (2048,), 20, 99991, jnp.int32), jax.random.randint(jax.random.fold_in(jax.random.fold_in(_rk, 5), 49), (2048,), 22, 12499, jnp.int32), jax.random.randint(jax.random.fold_in(jax.random.fold_in(_rk, 5), 50), (2048,), 31, 12495, jnp.int32), jax.random.randint(jax.random.fold_in(jax.random.fold_in(_rk, 5), 51), (2048,), 13, 99974, jnp.int32), jax.random.randint(jax.random.fold_in(jax.random.fold_in(_rk, 5), 52), (2048,), 4, 99972, jnp.int32), jax.random.randint(jax.random.fold_in(jax.random.fold_in(_rk, 5), 53), (2048,), 27, 99963, jnp.int32), jax.random.randint(jax.random.fold_in(jax.random.fold_in(_rk, 5), 54), (2048,), 17, 99999, jnp.int32), jax.random.randint(jax.random.fold_in(jax.random.fold_in(_rk, 5), 55), (2048,), 3, 99997, jnp.int32), jax.random.randint(jax.random.fold_in(jax.random.fold_in(_rk, 5), 56), (2048,), 15, 99958, jnp.int32), jax.random.randint(jax.random.fold_in(jax.random.fold_in(_rk, 5), 57), (2048,), 35, 12500, jnp.int32), jax.random.randint(jax.random.fold_in(jax.random.fold_in(_rk, 5), 58), (2048,), 44, 12494, jnp.int32), jax.random.randint(jax.random.fold_in(jax.random.fold_in(_rk, 5), 59), (2048,), 10, 99951, jnp.int32), jax.random.randint(jax.random.fold_in(jax.random.fold_in(_rk, 5), 60), (2048,), 9, 12495, jnp.int32), jax.random.randint(jax.random.fold_in(jax.random.fold_in(_rk, 5), 61), (2048,), 0, 99979, jnp.int32), jax.random.randint(jax.random.fold_in(jax.random.fold_in(_rk, 5), 62), (2048,), 36, 99965, jnp.int32), jax.random.randint(jax.random.fold_in(jax.random.fold_in(_rk, 5), 63), (2048,), 20, 99997, jnp.int32), jax.random.randint(jax.random.fold_in(jax.random.fold_in(_rk, 5), 64), (2048,), 54, 99994, jnp.int32), jax.random.randint(jax.random.fold_in(jax.random.fold_in(_rk, 5), 65), (2048,), 60, 99995, jnp.int32), jax.random.randint(jax.random.fold_in(jax.random.fold_in(_rk, 5), 66), (2048,), 10, 99951, jnp.int32), jax.random.randint(jax.random.fold_in(jax.random.fold_in(_rk, 5), 67), (2048,), 17, 99985, jnp.int32), jax.random.randint(jax.random.fold_in(jax.random.fold_in(_rk, 5), 68), (2048,), 0, 99998, jnp.int32), jax.random.randint(jax.random.fold_in(jax.random.fold_in(_rk, 5), 69), (2048,), 0, 99964, jnp.int32), jax.random.randint(jax.random.fold_in(jax.random.fold_in(_rk, 5), 70), (2048,), 68, 99970, jnp.int32), jax.random.randint(jax.random.fold_in(jax.random.fold_in(_rk, 5), 71), (2048,), 16, 99980, jnp.int32), jax.random.randint(jax.random.fold_in(jax.random.fold_in(_rk, 5), 72), (2048,), 6, 99994, jnp.int32), jax.random.randint(jax.random.fold_in(jax.random.fold_in(_rk, 5), 73), (2048,), 6, 99970, jnp.int32), jax.random.randint(jax.random.fold_in(jax.random.fold_in(_rk, 5), 74), (2048,), 6, 99997, jnp.int32), jax.random.randint(jax.random.fold_in(jax.random.fold_in(_rk, 5), 75), (2048,), 23, 99991, jnp.int32), jax.random.randint(jax.random.fold_in(jax.random.fold_in(_rk, 5), 76), (2048,), 133, 99975, jnp.int32), jax.random.randint(jax.random.fold_in(jax.random.fold_in(_rk, 5), 77), (2048,), 18, 99994, jnp.int32), jax.random.randint(jax.random.fold_in(jax.random.fold_in(_rk, 5), 78), (2048,), 43, 99898, jnp.int32), jax.random.randint(jax.random.fold_in(jax.random.fold_in(_rk, 5), 79), (2048,), 12, 99999, jnp.int32), jax.random.randint(jax.random.fold_in(jax.random.fold_in(_rk, 5), 80), (2048,), 7, 99983, jnp.int32), jax.random.randint(jax.random.fold_in(jax.random.fold_in(_rk, 5), 81), (2048,), 1, 99991, jnp.int32), jax.random.randint(jax.random.fold_in(jax.random.fold_in(_rk, 5), 82), (2048,), 28, 12500, jnp.int32), jax.random.randint(jax.random.fold_in(jax.random.fold_in(_rk, 5), 83), (2048,), 45, 99985, jnp.int32), jax.random.randint(jax.random.fold_in(jax.random.fold_in(_rk, 5), 84), (2048,), 16, 99975, jnp.int32), jax.random.randint(jax.random.fold_in(jax.random.fold_in(_rk, 5), 85), (2048,), 17, 99997, jnp.int32), jax.random.randint(jax.random.fold_in(jax.random.fold_in(_rk, 5), 86), (2048,), 3, 99999, jnp.int32), jax.random.randint(jax.random.fold_in(jax.random.fold_in(_rk, 5), 87), (2048,), 47, 99981, jnp.int32), jax.random.randint(jax.random.fold_in(jax.random.fold_in(_rk, 5), 88), (2048,), 41, 99962, jnp.int32), jax.random.randint(jax.random.fold_in(jax.random.fold_in(_rk, 5), 89), (2048,), 45, 99980, jnp.int32), jax.random.randint(jax.random.fold_in(jax.random.fold_in(_rk, 5), 90), (2048,), 1, 99969, jnp.int32), jax.random.randint(jax.random.fold_in(jax.random.fold_in(_rk, 5), 91), (2048,), 38, 99980, jnp.int32), jax.random.randint(jax.random.fold_in(jax.random.fold_in(_rk, 5), 92), (2048,), 6, 99986, jnp.int32), jax.random.randint(jax.random.fold_in(jax.random.fold_in(_rk, 5), 93), (2048,), 2, 99955, jnp.int32), jax.random.randint(jax.random.fold_in(jax.random.fold_in(_rk, 5), 94), (2048,), 9, 99988, jnp.int32), jax.random.randint(jax.random.fold_in(jax.random.fold_in(_rk, 5), 95), (2048,), 18, 99991, jnp.int32), jax.random.randint(jax.random.fold_in(jax.random.fold_in(_rk, 5), 96), (2048,), 24, 99948, jnp.int32), jax.random.randint(jax.random.fold_in(jax.random.fold_in(_rk, 5), 97), (2048,), 0, 99949, jnp.int32), jax.random.randint(jax.random.fold_in(jax.random.fold_in(_rk, 5), 98), (2048,), 22, 99977, jnp.int32), jax.random.randint(jax.random.fold_in(jax.random.fold_in(_rk, 5), 99), (2048,), 25, 99998, jnp.int32), jax.random.randint(jax.random.fold_in(jax.random.fold_in(_rk, 5), 100), (2048,), 33, 12500, jnp.int32), jax.random.randint(jax.random.fold_in(jax.random.fold_in(_rk, 5), 101), (2048,), 12, 99959, jnp.int32), jax.random.randint(jax.random.fold_in(jax.random.fold_in(_rk, 5), 102), (2048,), 28, 99977, jnp.int32), jax.random.randint(jax.random.fold_in(jax.random.fold_in(_rk, 5), 103), (2048,), 12, 99980, jnp.int32), jax.random.randint(jax.random.fold_in(jax.random.fold_in(_rk, 5), 104), (2048,), 62, 99945, jnp.int32), jax.random.randint(jax.random.fold_in(jax.random.fold_in(_rk, 5), 105), (2048,), 18, 99987, jnp.int32), jax.random.randint(jax.random.fold_in(jax.random.fold_in(_rk, 5), 106), (2048,), 53, 99988, jnp.int32), jax.random.randint(jax.random.fold_in(jax.random.fold_in(_rk, 5), 107), (2048,), 14, 99998, jnp.int32), jax.random.randint(jax.random.fold_in(jax.random.fold_in(_rk, 5), 108), (2048,), 29, 99962, jnp.int32), jax.random.randint(jax.random.fold_in(jax.random.fold_in(_rk, 5), 109), (2048,), 1, 99949, jnp.int32), jax.random.randint(jax.random.fold_in(jax.random.fold_in(_rk, 5), 110), (2048,), 20, 99997, jnp.int32), jax.random.randint(jax.random.fold_in(jax.random.fold_in(_rk, 5), 111), (2048,), 18, 12496, jnp.int32), jax.random.randint(jax.random.fold_in(jax.random.fold_in(_rk, 5), 112), (2048,), 26, 99959, jnp.int32), jax.random.randint(jax.random.fold_in(jax.random.fold_in(_rk, 5), 113), (2048,), 28, 12497, jnp.int32), jax.random.randint(jax.random.fold_in(jax.random.fold_in(_rk, 5), 114), (2048,), 38, 99898, jnp.int32), jax.random.randint(jax.random.fold_in(jax.random.fold_in(_rk, 5), 115), (2048,), 17, 99950, jnp.int32), jax.random.randint(jax.random.fold_in(jax.random.fold_in(_rk, 5), 116), (2048,), 3, 99993, jnp.int32), jax.random.randint(jax.random.fold_in(jax.random.fold_in(_rk, 5), 117), (2048,), 3, 99999, jnp.int32), jax.random.randint(jax.random.fold_in(jax.random.fold_in(_rk, 5), 118), (2048,), 15, 12493, jnp.int32), jax.random.randint(jax.random.fold_in(jax.random.fold_in(_rk, 5), 119), (2048,), 25, 99977, jnp.int32), jax.random.randint(jax.random.fold_in(jax.random.fold_in(_rk, 5), 120), (2048,), 4, 99998, jnp.int32), jax.random.randint(jax.random.fold_in(jax.random.fold_in(_rk, 5), 121), (2048,), 6, 99997, jnp.int32), jax.random.randint(jax.random.fold_in(jax.random.fold_in(_rk, 5), 122), (2048,), 17, 99983, jnp.int32), jax.random.randint(jax.random.fold_in(jax.random.fold_in(_rk, 5), 123), (2048,), 6, 99987, jnp.int32), jax.random.randint(jax.random.fold_in(jax.random.fold_in(_rk, 5), 124), (2048,), 88, 99939, jnp.int32), jax.random.randint(jax.random.fold_in(jax.random.fold_in(_rk, 5), 125), (2048,), 57, 12499, jnp.int32), jax.random.randint(jax.random.fold_in(jax.random.fold_in(_rk, 5), 126), (2048,), 34, 99970, jnp.int32), jax.random.randint(jax.random.fold_in(jax.random.fold_in(_rk, 5), 127), (2048,), 9, 99987, jnp.int32), jax.random.randint(jax.random.fold_in(jax.random.fold_in(_rk, 5), 128), (2048,), 0, 99996, jnp.int32), jax.random.randint(jax.random.fold_in(jax.random.fold_in(_rk, 5), 129), (2048,), 19, 12497, jnp.int32), jax.random.randint(jax.random.fold_in(jax.random.fold_in(_rk, 5), 130), (2048,), 44, 99995, jnp.int32), jax.random.randint(jax.random.fold_in(jax.random.fold_in(_rk, 5), 131), (2048,), 4, 99926, jnp.int32), jax.random.randint(jax.random.fold_in(jax.random.fold_in(_rk, 5), 132), (2048,), 13, 99999, jnp.int32), jax.random.randint(jax.random.fold_in(jax.random.fold_in(_rk, 5), 133), (2048,), 32, 99874, jnp.int32), jax.random.randint(jax.random.fold_in(jax.random.fold_in(_rk, 5), 134), (2048,), 3, 99986, jnp.int32), jax.random.randint(jax.random.fold_in(jax.random.fold_in(_rk, 5), 135), (2048,), 24, 99985, jnp.int32), jax.random.randint(jax.random.fold_in(jax.random.fold_in(_rk, 5), 136), (2048,), 18, 99995, jnp.int32), jax.random.randint(jax.random.fold_in(jax.random.fold_in(_rk, 5), 137), (2048,), 2, 99997, jnp.int32), jax.random.randint(jax.random.fold_in(jax.random.fold_in(_rk, 5), 138), (2048,), 14, 99993, jnp.int32), jax.random.randint(jax.random.fold_in(jax.random.fold_in(_rk, 5), 139), (2048,), 6, 99990, jnp.int32), jax.random.randint(jax.random.fold_in(jax.random.fold_in(_rk, 5), 140), (2048,), 0, 99980, jnp.int32), jax.random.randint(jax.random.fold_in(jax.random.fold_in(_rk, 5), 141), (2048,), 16, 99966, jnp.int32), jax.random.randint(jax.random.fold_in(jax.random.fold_in(_rk, 5), 142), (2048,), 37, 99990, jnp.int32), jax.random.randint(jax.random.fold_in(jax.random.fold_in(_rk, 5), 143), (2048,), 55, 99995, jnp.int32), jax.random.randint(jax.random.fold_in(jax.random.fold_in(_rk, 5), 144), (2048,), 26, 99906, jnp.int32), jax.random.randint(jax.random.fold_in(jax.random.fold_in(_rk, 5), 145), (2048,), 5, 99991, jnp.int32), jax.random.randint(jax.random.fold_in(jax.random.fold_in(_rk, 5), 146), (2048,), 37, 99961, jnp.int32), jax.random.randint(jax.random.fold_in(jax.random.fold_in(_rk, 5), 147), (2048,), 6, 99981, jnp.int32), jax.random.randint(jax.random.fold_in(jax.random.fold_in(_rk, 5), 148), (2048,), 21, 99998, jnp.int32), jax.random.randint(jax.random.fold_in(jax.random.fold_in(_rk, 5), 149), (2048,), 13, 99918, jnp.int32), jax.random.randint(jax.random.fold_in(jax.random.fold_in(_rk, 5), 150), (2048,), 9, 99973, jnp.int32), jax.random.randint(jax.random.fold_in(jax.random.fold_in(_rk, 5), 151), (2048,), 13, 99942, jnp.int32), jax.random.randint(jax.random.fold_in(jax.random.fold_in(_rk, 5), 152), (2048,), 5, 99986, jnp.int32), jax.random.randint(jax.random.fold_in(jax.random.fold_in(_rk, 5), 153), (2048,), 20, 99987, jnp.int32), jax.random.randint(jax.random.fold_in(jax.random.fold_in(_rk, 5), 154), (2048,), 21, 99986, jnp.int32), jax.random.randint(jax.random.fold_in(jax.random.fold_in(_rk, 5), 155), (2048,), 42, 99985, jnp.int32), jax.random.randint(jax.random.fold_in(jax.random.fold_in(_rk, 5), 156), (2048,), 33, 99975, jnp.int32), jax.random.randint(jax.random.fold_in(jax.random.fold_in(_rk, 5), 157), (2048,), 43, 99988, jnp.int32), jax.random.randint(jax.random.fold_in(jax.random.fold_in(_rk, 5), 158), (2048,), 11, 99937, jnp.int32), jax.random.randint(jax.random.fold_in(jax.random.fold_in(_rk, 5), 159), (2048,), 11, 99999, jnp.int32), jax.random.randint(jax.random.fold_in(jax.random.fold_in(_rk, 5), 160), (2048,), 15, 99989, jnp.int32), jax.random.randint(jax.random.fold_in(jax.random.fold_in(_rk, 5), 161), (2048,), 64, 99982, jnp.int32), jax.random.randint(jax.random.fold_in(jax.random.fold_in(_rk, 5), 162), (2048,), 53, 99994, jnp.int32), jax.random.randint(jax.random.fold_in(jax.random.fold_in(_rk, 5), 163), (2048,), 0, 99986, jnp.int32), jax.random.randint(jax.random.fold_in(jax.random.fold_in(_rk, 5), 164), (2048,), 89, 99994, jnp.int32), jax.random.randint(jax.random.fold_in(jax.random.fold_in(_rk, 5), 165), (2048,), 9, 99949, jnp.int32), jax.random.randint(jax.random.fold_in(jax.random.fold_in(_rk, 5), 166), (2048,), 30, 99889, jnp.int32), jax.random.randint(jax.random.fold_in(jax.random.fold_in(_rk, 5), 167), (2048,), 8, 99994, jnp.int32), jax.random.randint(jax.random.fold_in(jax.random.fold_in(_rk, 5), 168), (2048,), 23, 99868, jnp.int32), jax.random.randint(jax.random.fold_in(jax.random.fold_in(_rk, 5), 169), (2048,), 37, 99966, jnp.int32), jax.random.randint(jax.random.fold_in(jax.random.fold_in(_rk, 5), 170), (2048,), 100, 99994, jnp.int32), jax.random.randint(jax.random.fold_in(jax.random.fold_in(_rk, 5), 171), (2048,), 59, 99991, jnp.int32), jax.random.randint(jax.random.fold_in(jax.random.fold_in(_rk, 5), 172), (2048,), 9, 99961, jnp.int32), jax.random.randint(jax.random.fold_in(jax.random.fold_in(_rk, 5), 173), (2048,), 16, 12500, jnp.int32), jax.random.randint(jax.random.fold_in(jax.random.fold_in(_rk, 5), 174), (2048,), 32, 99995, jnp.int32), jax.random.randint(jax.random.fold_in(jax.random.fold_in(_rk, 5), 175), (2048,), 12, 99964, jnp.int32), jax.random.randint(jax.random.fold_in(jax.random.fold_in(_rk, 5), 176), (2048,), 41, 99987, jnp.int32), jax.random.randint(jax.random.fold_in(jax.random.fold_in(_rk, 5), 177), (2048,), 19, 99998, jnp.int32), jax.random.randint(jax.random.fold_in(jax.random.fold_in(_rk, 5), 178), (2048,), 25, 12497, jnp.int32), jax.random.randint(jax.random.fold_in(jax.random.fold_in(_rk, 5), 179), (2048,), 9, 99954, jnp.int32), jax.random.randint(jax.random.fold_in(jax.random.fold_in(_rk, 5), 180), (2048,), 43, 99926, jnp.int32), jax.random.randint(jax.random.fold_in(jax.random.fold_in(_rk, 5), 181), (2048,), 38, 99965, jnp.int32), jax.random.randint(jax.random.fold_in(jax.random.fold_in(_rk, 5), 182), (2048,), 5, 12500, jnp.int32), jax.random.randint(jax.random.fold_in(jax.random.fold_in(_rk, 5), 183), (2048,), 9, 99961, jnp.int32), jax.random.randint(jax.random.fold_in(jax.random.fold_in(_rk, 5), 184), (2048,), 15, 12499, jnp.int32), jax.random.randint(jax.random.fold_in(jax.random.fold_in(_rk, 5), 185), (2048,), 33, 12499, jnp.int32), jax.random.randint(jax.random.fold_in(jax.random.fold_in(_rk, 5), 186), (2048,), 29, 99979, jnp.int32), jax.random.randint(jax.random.fold_in(jax.random.fold_in(_rk, 5), 187), (2048,), 1, 99981, jnp.int32), jax.random.randint(jax.random.fold_in(jax.random.fold_in(_rk, 5), 188), (2048,), 11, 99987, jnp.int32), jax.random.randint(jax.random.fold_in(jax.random.fold_in(_rk, 5), 189), (2048,), 10, 99994, jnp.int32), jax.random.randint(jax.random.fold_in(jax.random.fold_in(_rk, 5), 190), (2048,), 13, 99996, jnp.int32), jax.random.randint(jax.random.fold_in(jax.random.fold_in(_rk, 5), 191), (2048,), 10, 99940, jnp.int32), jax.random.randint(jax.random.fold_in(jax.random.fold_in(_rk, 5), 192), (2048,), 11, 99995, jnp.int32), jax.random.randint(jax.random.fold_in(jax.random.fold_in(_rk, 5), 193), (2048,), 54, 99961, jnp.int32), jax.random.randint(jax.random.fold_in(jax.random.fold_in(_rk, 5), 194), (2048,), 20, 99996, jnp.int32), jax.random.randint(jax.random.fold_in(jax.random.fold_in(_rk, 5), 195), (2048,), 16, 99995, jnp.int32), jax.random.randint(jax.random.fold_in(jax.random.fold_in(_rk, 5), 196), (2048,), 12, 99994, jnp.int32), jax.random.randint(jax.random.fold_in(jax.random.fold_in(_rk, 5), 197), (2048,), 19, 99977, jnp.int32), jax.random.randint(jax.random.fold_in(jax.random.fold_in(_rk, 5), 198), (2048,), 0, 99983, jnp.int32), jax.random.randint(jax.random.fold_in(jax.random.fold_in(_rk, 5), 199), (2048,), 27, 99999, jnp.int32)], axis=1)
        r_seq_lengths = jax.random.randint(jax.random.fold_in(_rk, 6), (2048,), 1, 201, jnp.int32)
        return (r_user_id, r_target_tag, r_target_artist, r_hist_tags, r_hist_artists, r_seq_lengths)
    r_user_id, r_target_tag, r_target_artist, r_hist_tags, r_hist_artists, r_seq_lengths = _rec_inputs()

    def _L0_rec_setup():
        import jax, jax.numpy as jnp
        import numpy as np
        B, T, E = (512, 200, 64)
        N_USER = N_TAG = N_ARTIST = 12500

        def prelu(x, a):
            return jnp.where(x >= 0, x, a * x)
        key = jax.random.key(seed)
        ks = jax.random.split(key, 24)
        d = {}
        d['user_id'] = jax.random.randint(ks[0], (B,), 0, N_USER)
        d['target_tag'] = jax.random.randint(ks[1], (B,), 0, N_TAG)
        d['target_artist'] = jax.random.randint(ks[2], (B,), 0, N_ARTIST)
        d['hist_tags'] = jax.random.randint(ks[3], (B, T), 0, N_TAG)
        d['hist_artists'] = jax.random.randint(ks[4], (B, T), 0, N_ARTIST)
        d['hist_weights'] = jax.random.uniform(ks[5], (B, T), dtype=jnp.float32)
        d['seq_lengths'] = jax.random.randint(ks[6], (B,), 1, T + 1)
        d['user_table'] = 0.01 * jax.random.normal(ks[7], (N_USER, E), dtype=jnp.float32)
        d['tag_table'] = 0.01 * jax.random.normal(ks[8], (N_TAG, E), dtype=jnp.float32)
        d['artist_table'] = 0.01 * jax.random.normal(ks[9], (N_ARTIST, E), dtype=jnp.float32)

        def lin(k, out_d, in_d):
            return jax.random.normal(k, (out_d, in_d), dtype=jnp.float32) * np.sqrt(2.0 / in_d)
        d['att_w0'] = lin(ks[10], 80, 4 * E)
        d['att_b0'] = jnp.zeros((80,), jnp.float32)
        d['att_a0'] = jnp.full((1,), 0.25, jnp.float32)
        d['att_w1'] = lin(ks[11], 40, 80)
        d['att_b1'] = jnp.zeros((40,), jnp.float32)
        d['att_a1'] = jnp.full((1,), 0.25, jnp.float32)
        d['att_w2'] = lin(ks[12], 1, 40)
        d['att_b2'] = jnp.zeros((1,), jnp.float32)
        d['mlp_w0'] = lin(ks[13], 128, 4 * E)
        d['mlp_b0'] = jnp.zeros((128,), jnp.float32)
        d['mlp_a0'] = jnp.full((1,), 0.25, jnp.float32)
        d['mlp_w1'] = lin(ks[14], 64, 128)
        d['mlp_b1'] = jnp.zeros((64,), jnp.float32)
        d['mlp_a1'] = jnp.full((1,), 0.25, jnp.float32)
        d['mlp_w2'] = lin(ks[15], 1, 64)
        d['mlp_b2'] = jnp.zeros((1,), jnp.float32)
        return d
    _L0_rec_all = _L0_rec_setup()
    _L0_rec_in = {k: v for k, v in _L0_rec_all.items() if k in ('hist_weights', 'user_table', 'tag_table', 'artist_table', 'att_w0', 'att_b0', 'att_a0', 'att_w1', 'att_b1', 'att_a1', 'att_w2', 'att_b2', 'mlp_w0', 'mlp_b0', 'mlp_a0', 'mlp_w1', 'mlp_b1', 'mlp_a1', 'mlp_w2', 'mlp_b2')}
    del _L0_rec_all
    return {'r_user_id': r_user_id, 'r_target_tag': r_target_tag, 'r_target_artist': r_target_artist, 'r_hist_tags': r_hist_tags, 'r_hist_artists': r_hist_artists, 'r_seq_lengths': r_seq_lengths, 'L0_rec_hist_weights': _L0_rec_in['hist_weights'], 'L0_rec_user_table': _L0_rec_in['user_table'], 'L0_rec_tag_table': _L0_rec_in['tag_table'], 'L0_rec_artist_table': _L0_rec_in['artist_table'], 'L0_rec_att_w0': _L0_rec_in['att_w0'], 'L0_rec_att_b0': _L0_rec_in['att_b0'], 'L0_rec_att_a0': _L0_rec_in['att_a0'], 'L0_rec_att_w1': _L0_rec_in['att_w1'], 'L0_rec_att_b1': _L0_rec_in['att_b1'], 'L0_rec_att_a1': _L0_rec_in['att_a1'], 'L0_rec_att_w2': _L0_rec_in['att_w2'], 'L0_rec_att_b2': _L0_rec_in['att_b2'], 'L0_rec_mlp_w0': _L0_rec_in['mlp_w0'], 'L0_rec_mlp_b0': _L0_rec_in['mlp_b0'], 'L0_rec_mlp_a0': _L0_rec_in['mlp_a0'], 'L0_rec_mlp_w1': _L0_rec_in['mlp_w1'], 'L0_rec_mlp_b1': _L0_rec_in['mlp_b1'], 'L0_rec_mlp_a1': _L0_rec_in['mlp_a1'], 'L0_rec_mlp_w2': _L0_rec_in['mlp_w2'], 'L0_rec_mlp_b2': _L0_rec_in['mlp_b2']}

def reference(r_user_id, r_target_tag, r_target_artist, r_hist_tags, r_hist_artists, r_seq_lengths, L0_rec_hist_weights, L0_rec_user_table, L0_rec_tag_table, L0_rec_artist_table, L0_rec_att_w0, L0_rec_att_b0, L0_rec_att_a0, L0_rec_att_w1, L0_rec_att_b1, L0_rec_att_a1, L0_rec_att_w2, L0_rec_att_b2, L0_rec_mlp_w0, L0_rec_mlp_b0, L0_rec_mlp_a0, L0_rec_mlp_w1, L0_rec_mlp_b1, L0_rec_mlp_a1, L0_rec_mlp_w2, L0_rec_mlp_b2):
    import jax
    import jax.numpy as jnp

    def _L0_rec_ref(user_id, target_tag, target_artist, hist_tags, hist_artists, hist_weights, seq_lengths, user_table, tag_table, artist_table, att_w0, att_b0, att_a0, att_w1, att_b1, att_a1, att_w2, att_b2, mlp_w0, mlp_b0, mlp_a0, mlp_w1, mlp_b1, mlp_a1, mlp_w2, mlp_b2):
        import jax, jax.numpy as jnp
        import numpy as np
        B, T, E = (512, 200, 64)
        N_USER = N_TAG = N_ARTIST = 12500

        def prelu(x, a):
            return jnp.where(x >= 0, x, a * x)
        user_emb = user_table[user_id]
        q = tag_table[target_tag]
        target_artist_emb = artist_table[target_artist]
        keys = tag_table[hist_tags] + artist_table[hist_artists]
        qx = jnp.broadcast_to(q[:, None, :], keys.shape)
        att_in = jnp.concatenate([qx, keys, qx - keys, qx * keys], axis=-1)
        h = prelu(jnp.einsum('bti,oi->bto', att_in, att_w0) + att_b0, att_a0)
        h = prelu(jnp.einsum('bti,oi->bto', h, att_w1) + att_b1, att_a1)
        score = (jnp.einsum('bti,oi->bto', h, att_w2) + att_b2)[..., 0]
        mask = jnp.arange(T)[None, :] < seq_lengths[:, None]
        score = jnp.where(mask, score, -1000000000.0)
        att = jax.nn.softmax(score, axis=1)
        hist_att = jnp.einsum('bt,bte->be', att, keys)
        feat = jnp.concatenate([user_emb, q, target_artist_emb, hist_att], axis=1)
        z = prelu(feat @ mlp_w0.T + mlp_b0, mlp_a0)
        z = prelu(z @ mlp_w1.T + mlp_b1, mlp_a1)
        z = (z @ mlp_w2.T + mlp_b2)[:, 0]
        return jax.nn.sigmoid(z)
    y = _L0_rec_ref(r_user_id, r_target_tag, r_target_artist, r_hist_tags, r_hist_artists, L0_rec_hist_weights, r_seq_lengths, L0_rec_user_table, L0_rec_tag_table, L0_rec_artist_table, L0_rec_att_w0, L0_rec_att_b0, L0_rec_att_a0, L0_rec_att_w1, L0_rec_att_b1, L0_rec_att_a1, L0_rec_att_w2, L0_rec_att_b2, L0_rec_mlp_w0, L0_rec_mlp_b0, L0_rec_mlp_a0, L0_rec_mlp_w1, L0_rec_mlp_b1, L0_rec_mlp_a1, L0_rec_mlp_w2, L0_rec_mlp_b2)
    return y

_drawn_inputs = setup_inputs


def setup_inputs(seed=0):
    import zlib

    import numpy as np

    out = dict(_drawn_inputs(seed))
    spreads = {'L0_rec_att_b0': (0.0, 0.8),
     'L0_rec_att_b1': (0.0, 0.8),
     'L0_rec_mlp_b0': (0.0, 0.8),
     'L0_rec_mlp_b1': (0.0, 0.1)}
    factors = {'L0_rec_user_table': 8.0,
     'L0_rec_tag_table': 8.0,
     'L0_rec_artist_table': 8.0,
     'L0_rec_att_w0': 8.0,
     'L0_rec_att_w1': 8.0,
     'L0_rec_att_w2': 8.0,
     'L0_rec_mlp_w0': 8.0,
     'L0_rec_mlp_w2': 4.226}
    for name, (base, spread) in spreads.items():
        noise = np.random.default_rng([zlib.crc32(name.encode()), seed]).standard_normal(out[name].shape)
        drawn = base * np.exp(spread * noise) if base else spread * noise
        out[name] = jnp.asarray(drawn.astype(out[name].dtype))
    for name, factor in factors.items():
        out[name] = (out[name] * factor).astype(out[name].dtype)
    return out
```

```python
from contextlib import ExitStack

import concourse.bass as bass
from concourse import mybir

F32 = mybir.dt.float32
I32 = mybir.dt.int32
U32 = mybir.dt.uint32
ALU = mybir.AluOpType
ACT = mybir.ActivationFunctionType
AX_X = mybir.AxisListType.X

P = 128
CHUNK = 4
SLOTS = 2
PASS = CHUNK * SLOTS
MASKED = -1000000000.0
HUGE = 3.0e38
META = 8


def program(nc, lengths, rows, user_table, tag_table, artist_table, a_w0, a_b0, a_a0, a_w1, a_b1, a_a1,
            a_w2, a_b2, m_w0, m_b0, m_a0, m_w1, m_b1, m_a1, m_w2, m_b2, sorted_rows, out):
    B, ROW = rows.shape
    T = ROW - META
    N, E = tag_table.shape
    GROUPS = B // P
    H0, H1 = a_w0.shape[1], a_w1.shape[1]
    M0, M1 = m_w0.shape[1], m_w1.shape[1]
    T //= 2
    PASSES = T // PASS
    COLS = CHUNK * P
    ONE0 = 96
    ONE1 = 64
    W = E + 1
    assert user_table.shape[0] == N and artist_table.shape[0] == N
    assert 2 * E == P and T % PASS == 0 and H0 <= ONE0 and H1 < ONE1 and M1 == ONE1

    with ExitStack() as ctx:
        def sb(name, shape, dt=F32):
            return ctx.enter_context(nc.sbuf_tensor(name, shape, dt))

        def ps(name, shape):
            return ctx.enter_context(nc.psum_tensor(name, shape, F32))

        def sem(name):
            return ctx.enter_context(nc.semaphore(name))

        def sems(name):
            return [sem(f"{name}{k}") for k in range(SLOTS)]

        len_row = sb("len_row", [P, B], I32)
        len_own = sb("len_own", [P, GROUPS], I32)
        tie_row = sb("tie_row", [P, B])
        tie_own = sb("tie_own", [P, GROUPS])
        key_row = sb("key_row", [P, B])
        key_own = sb("key_own", [P, GROUPS])
        full_row = sb("full_row", [P, B])
        full_own = sb("full_own", [P, GROUPS])
        beats = sb("beats", [P, B])
        rank_f = sb("rank_f", [P, GROUPS])
        rank = sb("rank", [P, GROUPS], U32)
        row_sb = sb("row_sb", [P, GROUPS, ROW], I32)
        wrap = sb("wrap", [P, ROW], I32)
        lead = sb("lead", [1, GROUPS], I32)
        lead_f = sb("lead_f", [1, GROUPS])
        lead_full = sb("lead_full", [1, GROUPS])
        pass_start = sb("pass_start", [1, PASSES])
        pass_used = sb("pass_used", [1, GROUPS, PASSES])
        n_pass = sb("n_pass", [1, GROUPS])
        zeros16 = sb("zeros16", [1, GROUPS])
        spare = sb("spare", [1, 8])
        pass_end = sb("pass_end", [1, GROUPS])
        first_pass = sb("first_pass", [1, GROUPS + 1], I32)
        perm = sb("perm", [P, GROUPS], I32)

        ident = sb("ident", [P, P])
        w_keys = sb("w_keys", [P, H0])
        w_diff_hi = sb("w_diff_hi", [P, H0])
        w_q = sb("w_q", [E + 1, H0])
        w_diff_lo = sb("w_diff_lo", [E, H0])
        w_1 = sb("w_1", [ONE0 + 1, H1])
        w_2 = sb("w_2", [ONE1 + 1, 1])
        slopes = sb("slopes", [P, 4])
        coslopes = sb("coslopes", [P, 4])
        mw_0 = sb("mw_0", [P, 2, M0])
        mb_0 = sb("mb_0", [M0, 1])
        mw_1 = sb("mw_1", [M0, M1])
        mb_1 = sb("mb_1", [M1, 1])
        mw_2 = sb("mw_2", [M1 + 1, 1])

        head_idx = sb("head_idx", [P, META], I32)
        head = sb("head", [P, 3, E])
        q_cur = sb("q_cur", [P, E])
        q_t = sb("q_t", [E + 1, P])
        left = sb("left", [P, 1])
        inv_sum = sb("inv_sum", [P, 1])
        feat = sb("feat", [P, GROUPS, 4 * E])

        stage = [sb(f"stage{k}", [P, 2 * CHUNK], I32) for k in range(SLOTS)]
        got = [sb(f"got{k}", [P, 2, CHUNK, E]) for k in range(SLOTS)]
        keys = [sb(f"keys{k}", [P, CHUNK + 1, P + 1]) for k in range(SLOTS)]
        keys_t = [sb(f"keys_t{k}", [P, COLS]) for k in range(SLOTS)]
        neg_0 = [sb(f"neg_0{k}", [H0, COLS]) for k in range(SLOTS)]
        hid_0 = [sb(f"hid_0{k}", [ONE0 + 1, COLS]) for k in range(SLOTS)]
        neg_1 = [sb(f"neg_1{k}", [H1, COLS]) for k in range(SLOTS)]
        hid_1 = [sb(f"hid_1{k}", [ONE1 + 1, COLS]) for k in range(SLOTS)]
        place = [sb(f"place{k}", [P, CHUNK]) for k in range(SLOTS)]
        open_ = [sb(f"open{k}", [P, CHUNK]) for k in range(SLOTS)]
        score = [sb(f"score{k}", [P, CHUNK + 1]) for k in range(SLOTS)]
        below = [sb(f"below{k}", [P, CHUNK + 1]) for k in range(SLOTS)]
        prob = [sb(f"prob{k}", [P, CHUNK + 1]) for k in range(SLOTS)]
        part = [sb(f"part{k}", [P, CHUNK + 1, W]) for k in range(SLOTS)]

        feat_t = sb("feat_t", [P, 2, COLS])
        mx_0 = sb("mx_0", [M0, COLS])
        mneg_0 = sb("mneg_0", [M0, COLS])
        mhid_0 = sb("mhid_0", [M0, COLS])
        mx_1 = sb("mx_1", [M1, COLS])
        mneg_1 = sb("mneg_1", [M1, COLS])
        mhid_1 = sb("mhid_1", [M1 + 1, COLS])
        result = sb("result", [P, GROUPS])

        p_t = [ps(f"p_t{k}", [P, COLS]) for k in range(SLOTS)]
        p_0 = [ps(f"p_0{k}", [P, COLS]) for k in range(SLOTS)]
        p_1 = [ps(f"p_1{k}", [P, COLS]) for k in range(SLOTS)]
        p_s = ps("p_s", [P, COLS])
        p_q = ps("p_q", [P, COLS])

        s_len = sem("s_len")
        s_rows = sem("s_rows")
        s_const = sem("s_const")
        s_key = sem("s_key")
        s_rank = sem("s_rank")
        s_clamp = sem("s_clamp")
        s_scattered = sem("s_scattered")
        s_lead = sem("s_lead")
        s_plan = sem("s_plan")
        s_planned = sem("s_planned")
        s_perm = sem("s_perm")
        s_zeroed = sem("s_zeroed")
        s_weights = sem("s_weights")
        s_wprep = sem("s_wprep")
        s_ones = sem("s_ones")

        s_head_idx = sem("s_head_idx")
        s_head = sem("s_head")
        s_head_used = sem("s_head_used")
        s_head_sent = sem("s_head_sent")
        s_q_cur = sem("s_q_cur")
        s_q_turned = sem("s_q_turned")
        s_q_t = sem("s_q_t")
        s_state = sem("s_state")
        s_left = sem("s_left")
        s_inv = sem("s_inv")
        s_group = sem("s_group")

        s_stage = sems("s_stage")
        s_got = sems("s_got")
        s_summed = sems("s_summed")
        s_keys = sems("s_keys")
        s_turned = sems("s_turned")
        s_keys_t = sems("s_keys_t")
        s_l0 = sems("s_l0")
        s_neg0 = sems("s_neg0")
        s_hid0 = sems("s_hid0")
        s_l1 = sems("s_l1")
        s_neg1 = sems("s_neg1")
        s_hid1 = sems("s_hid1")
        s_l2 = sems("s_l2")
        s_open = sems("s_open")
        s_masked = sems("s_masked")
        s_max = sems("s_max")
        s_below = sems("s_below")
        s_prob = sems("s_prob")
        s_part = sems("s_part")
        s_sum = sems("s_sum")

        s_mlp_pe = sem("s_mlp_pe")
        s_mlp_act = sem("s_mlp_act")
        s_mlp_dve = sem("s_mlp_dve")
        s_result = sem("s_result")
        s_out = sem("s_out")

        NW = 17

        block = ctx.enter_context(nc.Block())

        def passes(eng, g):
            a = eng.value_load(first_pass[0:1, bass.ds(g, 1)], min_val=0, max_val=GROUPS * PASSES)
            b = eng.value_load(first_pass[0:1, bass.ds(g + 1, 1)], min_val=0, max_val=GROUPS * PASSES)
            return a, b

        @block.sync
        def _(sp):
            sp.dma_start(len_row[:, :], lengths.partition_broadcast(P)).then_inc(s_len, 16)
            sp.dma_start(len_own[:, :], lengths.rearrange("(p j) -> p j", p=P)).then_inc(s_len, 16)
            sp.dma_start(row_sb[:, :, :], rows.rearrange("(p j) c -> p j c", p=P)).then_inc(s_rows, 16)

            sp.wait_ge(s_scattered, 16 * GROUPS)
            by_group = sorted_rows.rearrange("(g p) c -> p g c", p=P)
            with nc.allow_non_contiguous_dma(reason="one word per group"):
                sp.dma_start(lead[:, :], by_group[0:1, :, 2 * T]).then_inc(s_lead, 16)
                sp.dma_start(perm[:, :], by_group[:, :, 2 * T + 4]).then_inc(s_perm, 16)

            sp.wait_ge(s_planned, 1)
            with sp.Fori(0, GROUPS) as g:
                first, end = passes(sp, g)
                sp.wait_ge(s_head_used, g + 1)
                sp.dma_start(head_idx[:, :], sorted_rows[bass.ds(g * P, P), 2 * T:2 * T + META]) \
                    .then_inc(s_head_idx, 16)
                with sp.Fori(first, end) as i:
                    at = nc.s_assert_within((i - first) * (2 * PASS), 0, (PASSES - 1) * (2 * PASS))
                    for k in range(SLOTS):
                        sp.wait_ge(s_summed[k], i + 1)
                        sp.dma_start(stage[k][:, :],
                                     sorted_rows[bass.ds(g * P, P),
                                                 bass.ds(at + 2 * CHUNK * k, 2 * CHUNK)]) \
                            .then_inc(s_stage[k], 16)

        @block.gpsimd
        def _(pool):
            pool.iota(tie_row[:, :], [[-1, B]], base=B - 1, channel_multiplier=0,
                      allow_small_or_imprecise_dtypes=True).then_inc(s_const, 1)
            pool.iota(tie_own[:, :], [[-1, GROUPS]], base=B - 1, channel_multiplier=-GROUPS,
                      allow_small_or_imprecise_dtypes=True).then_inc(s_const, 1)
            pool.iota(pass_start[:, :], [[PASS, PASSES]], base=0, channel_multiplier=0,
                      allow_small_or_imprecise_dtypes=True).then_inc(s_const, 1)
            for k in range(SLOTS):
                pool.iota(place[k][:, :], [[1, CHUNK]], base=CHUNK * k, channel_multiplier=0,
                          allow_small_or_imprecise_dtypes=True).then_inc(s_const, 1)
            pool.memset(ident[:, :], 0.0).then_inc(s_const, 1)
            pool.wait_ge(s_const, 6)
            pool.affine_select(out=ident[:, :], in_=ident[:, :], compare_op=ALU.not_equal, fill=1.0,
                               base=0, pattern=[[-1, P]], channel_multiplier=1).then_inc(s_const, 1)
            pool.wait_ge(s_rows, 16)
            for j in range(GROUPS):
                for n, (lo, hi) in enumerate(((0, 2 * T), (2 * T + 1, 2 * T + 4))):
                    x, y = row_sb[:, j, lo:hi], wrap[:, lo:hi]
                    at = 3 * (2 * j + n)
                    pool.tensor_scalar(y, x, 0.0, float(N), ALU.is_lt, ALU.mult).then_inc(s_clamp, 1)
                    pool.wait_ge(s_clamp, at + 1)
                    pool.tensor_tensor(x, x, y, ALU.add).then_inc(s_clamp, 1)
                    pool.wait_ge(s_clamp, at + 2)
                    pool.tensor_scalar(x, x, 0.0, float(N - 1), ALU.max, ALU.min).then_inc(s_clamp, 1)
            pool.wait_ge(s_clamp, 6 * GROUPS)
            pool.wait_ge(s_rank, 1)
            for j in range(GROUPS):
                pool.indirect_dma_start(
                    out=sorted_rows, out_offset=bass.IndirectOffsetOnAxis(ap=rank[:, j:j + 1], axis=0),
                    in_=row_sb[:, j, :], in_offset=None).then_inc(s_scattered, 16)

            head_loads, turn, loads = (pool.alloc_register(name) for name in ("head_loads", "turn", "loads"))
            for register in (head_loads, turn, loads):
                pool.reg_mov(register, 0)
            pool.wait_ge(s_planned, 1)
            with pool.Fori(0, GROUPS) as g:
                first, end = passes(pool, g)
                pool.reg_add(head_loads, head_loads, 16)
                pool.wait_ge(s_planned, 1)
                pool.wait_ge(s_head_idx, head_loads)
                for n, (table, col) in enumerate(((user_table, 1), (tag_table, 2), (artist_table, 3))):
                    pool.indirect_dma_start(
                        out=head[:, n, :], out_offset=None, in_=table,
                        in_offset=bass.IndirectOffsetOnAxis(ap=head_idx[:, col:col + 1].bitcast(U32), axis=0)) \
                        .then_inc(s_head, 16)
                with pool.Fori(first, end) as i:
                    pool.reg_add(turn, turn, 1)
                    pool.reg_add(loads, loads, 16)
                    for k in range(SLOTS):
                        pool.wait_ge(s_planned, 1)
                        pool.wait_ge(s_stage[k], loads)
                        pool.wait_ge(s_summed[k], turn)
                        for n, table in enumerate((tag_table, artist_table)):
                            for t in range(CHUNK):
                                c = n * CHUNK + t
                                pool.indirect_dma_start(
                                    out=got[k][:, n, t, :], out_offset=None, in_=table,
                                    in_offset=bass.IndirectOffsetOnAxis(
                                        ap=stage[k][:, c:c + 1].bitcast(U32), axis=0)).then_inc(s_got[k], 16)
            pool.wait_ge(s_perm, 16)
            pool.wait_ge(s_result, 1)
            for g in range(GROUPS):
                pool.indirect_dma_start(
                    out=out, out_offset=bass.IndirectOffsetOnAxis(ap=perm[:, g:g + 1].bitcast(U32), axis=0),
                    in_=result[:, g:g + 1], in_offset=None).then_inc(s_out, 16)
            pool.wait_ge(s_out, 16 * GROUPS)

        @block.scalar
        def _(act):
            act.wait_ge(s_zeroed, 1)
            loads = [
                (w_keys[0:E, :], a_w0[3 * E:4 * E, :]), (w_keys[E:P, :], a_w0[E:2 * E, :]),
                (w_diff_hi[E:P, :], a_w0[2 * E:3 * E, :]), (w_diff_lo[:, :], a_w0[2 * E:3 * E, :]),
                (w_q[0:E, :], a_w0[0:E, :]), (w_q[E:E + 1, :], a_b0),
                (w_1[0:H0, :], a_w1), (w_1[ONE0:ONE0 + 1, :], a_b1),
                (w_2[0:H1, :], a_w2), (w_2[ONE1:ONE1 + 1, :], a_b2),
                (mw_0[:, :, :], m_w0.rearrange("(h k) n -> k h n", h=2)), (mw_1[:, :], m_w1),
                (mw_2[0:M1, :], m_w2), (mw_2[M1:M1 + 1, :], m_b2),
                (mb_0[:, :], m_b0), (mb_1[:, :], m_b1),
            ]
            for dst, src in loads:
                act.dma_start(dst, src).then_inc(s_weights, 16)
            for n, a in enumerate((a_a0, a_a1, m_a0, m_a1)):
                act.dma_start(slopes[:, n:n + 1], a.partition_broadcast(P)).then_inc(s_weights, 16)

            def turn(k, i):
                act.wait_ge(s_turned[k], i + 1)
                act.activation(keys_t[k][:, :], p_t[k][:, :], ACT.Copy).then_inc(s_keys_t[k], 1)

            def relu0(k, i):
                act.wait_ge(s_l0[k], i + 1)
                act.activation(neg_0[k][:, :], p_0[k][0:H0, :], ACT.Relu, scale=-1.0).then_inc(s_neg0[k], 1)

            def relu1(k, i):
                act.wait_ge(s_l1[k], i + 1)
                act.activation(neg_1[k][:, :], p_1[k][0:H1, :], ACT.Relu, scale=-1.0).then_inc(s_neg1[k], 1)

            def exp(k, i):
                act.wait_ge(s_below[k], i + 1)
                act.activation(prob[k][:, :], below[k][:, :], ACT.Exp).then_inc(s_prob[k], 1)

            def step(k, i, before):
                if before:
                    relu1(*before)
                turn(k, i)
                if before:
                    exp(*before)
                relu0(k, i)

            act.wait_ge(s_planned, 1)
            with act.Fori(0, GROUPS) as g:
                first, end = passes(act, g)
                act.wait_ge(s_q_turned, g + 1)
                act.activation(q_t[0:E, :], p_q[0:E, 0:P], ACT.Copy).then_inc(s_q_t, 1)
                step(0, first, None)
                step(1, first, (0, first))
                with act.Fori(first + 1, end) as i:
                    step(0, i, (1, i - 1))
                    step(1, i, (0, i))
                relu1(1, end - 1)
                exp(1, end - 1)

            n_pe = n_dve = 0
            for b in range(B // COLS):
                for h in range(2):
                    n_pe += 1
                    act.wait_ge(s_mlp_pe, n_pe)
                    act.activation(feat_t[:, h, :], p_t[h][:, :], ACT.Copy).then_inc(s_mlp_act, 1)
                for neg, x in ((mneg_0, mx_0), (mneg_1, mx_1)):
                    act.wait_ge(s_mlp_dve, n_dve + 1)
                    act.activation(neg[:, :], x[:, :], ACT.Relu, scale=-1.0).then_inc(s_mlp_act, 1)
                    n_dve += 2
                n_pe += 3
            act.wait_ge(s_mlp_pe, n_pe)
            act.activation(result[:, :], p_s[:, 0:GROUPS], ACT.Sigmoid).then_inc(s_result, 1)

        @block.tensor
        def _(pe):
            pe.wait_ge(s_const, 7)
            pe.wait_ge(s_wprep, 2)
            pe.wait_ge(s_ones, 1)

            def turn(k, i):
                pe.wait_ge(s_keys[k], i + 1)
                for t in range(CHUNK):
                    mm = pe.transpose(p_t[k][:, t * P:(t + 1) * P], keys[k][:, t, 0:P], ident[:, :])
                mm.then_inc(s_turned[k], 1)

            def layer0(k, i):
                pe.matmul(p_0[k][0:H0, :], w_q[:, :], q_t[:, :].unsqueeze(1).broadcast_to([E + 1, CHUNK, P]),
                          start=True, stop=False)
                pe.wait_ge(s_keys_t[k], i + 1)
                pe.matmul(p_0[k][0:H0, :], w_keys[:, :], keys_t[k][:, :],
                          start=False, stop=True).then_inc(s_l0[k], 1)

            def layer1(k, i):
                pe.wait_ge(s_hid0[k], i + 1)
                pe.matmul(p_1[k][0:H1, :], w_1[:, :], hid_0[k][:, :], start=True, stop=True).then_inc(s_l1[k], 1)

            def layer2(k, i):
                pe.wait_ge(s_hid1[k], i + 1)
                for t in range(CHUNK):
                    c = k * CHUNK + t
                    mm = pe.matmul(p_s[:, c:c + 1], hid_1[k][:, t * P:(t + 1) * P], w_2[:, :],
                                   start=True, stop=True)
                mm.then_inc(s_l2[k], 1)

            def step(k, i, before):
                turn(k, i)
                if before:
                    layer2(*before)
                layer0(k, i)
                layer1(k, i)

            pe.wait_ge(s_planned, 1)
            with pe.Fori(0, GROUPS) as g:
                first, end = passes(pe, g)
                pe.wait_ge(s_planned, 1)
                pe.wait_ge(s_q_cur, g + 1)
                pe.transpose(p_q[0:E, 0:P], q_cur[:, :], ident[:, :]).then_inc(s_q_turned, 1)
                pe.wait_ge(s_q_t, g + 1)
                step(0, first, None)
                step(1, first, (0, first))
                with pe.Fori(first + 1, end) as i:
                    step(0, i, (1, i - 1))
                    step(1, i, (0, i))
                layer2(1, end - 1)

            pe.wait_ge(s_group, GROUPS + 1)
            n_act = n_dve = 0
            for b in range(B // COLS):
                for h in range(2):
                    for g in range(CHUNK):
                        mm = pe.transpose(p_t[h][:, g * P:(g + 1) * P],
                                          feat[:, b * CHUNK + g, h * P:(h + 1) * P], ident[:, :])
                    mm.then_inc(s_mlp_pe, 1)
                n_act += 2
                pe.wait_ge(s_mlp_act, n_act)
                for h in range(2):
                    mm = pe.matmul(p_0[0][0:M0, :], mw_0[:, h, :], feat_t[:, h, :], start=h == 0, stop=h == 1)
                mm.then_inc(s_mlp_pe, 1)
                n_dve += 2
                pe.wait_ge(s_mlp_dve, n_dve)
                pe.matmul(p_1[0][0:M1, :], mw_1[:, :], mhid_0[:, :], start=True, stop=True).then_inc(s_mlp_pe, 1)
                n_dve += 2
                pe.wait_ge(s_mlp_dve, n_dve)
                n_act += 2
                for g in range(CHUNK):
                    c = b * CHUNK + g
                    mm = pe.matmul(p_s[:, c:c + 1], mhid_1[:, g * P:(g + 1) * P], mw_2[:, :],
                                   start=True, stop=True)
                mm.then_inc(s_mlp_pe, 1)

        @block.vector
        def _(dve):
            for tile in (w_1, w_2, hid_0[0], hid_0[1], hid_1[0], hid_1[1]):
                ins = dve.memset(tile[:, :], 0.0)
            ins.then_inc(s_zeroed, 1)
            dve.wait_ge(s_zeroed, 1)
            for tile, row in ((hid_0[0], ONE0), (hid_0[1], ONE0), (hid_1[0], ONE1), (hid_1[1], ONE1),
                              (q_t, E), (mhid_1, M1)):
                dve.memset(tile[row:row + 1, :], 1.0)
            for k in range(SLOTS):
                dve.memset(keys[k][:, :, P:P + 1], 1.0)
            dve.memset(zeros16[:, :], 0.0).then_inc(s_ones, 1)

            dve.wait_ge(s_len, 32)
            dve.wait_ge(s_const, 5)
            n = 0
            for ln, full, tie, key in ((len_row, full_row, tie_row, key_row), (len_own, full_own, tie_own, key_own)):
                dve.tensor_scalar(full[:, :], ln[:, :], 0.0, float(T), ALU.is_le, ALU.mult).then_inc(s_key, 1)
                dve.tensor_scalar(key[:, :], ln[:, :], 0.0, float(T), ALU.max, ALU.min).then_inc(s_key, 1)
                n += 2
                dve.wait_ge(s_key, n)
                dve.tensor_tensor(full[:, :], full[:, :], key[:, :], ALU.add).then_inc(s_key, 1)
                n += 1
                dve.wait_ge(s_key, n)
                dve.scalar_tensor_tensor(key[:, :], full[:, :], float(B), tie[:, :], ALU.mult, ALU.add) \
                    .then_inc(s_key, 1)
                n += 1
            dve.wait_ge(s_key, n)
            for j in range(GROUPS):
                dve.tensor_scalar(beats[:, :], key_row[:, :], key_own[:, j:j + 1], 0.0, ALU.is_gt, ALU.add,
                                  accum_out=rank_f[:, j:j + 1]).then_inc(s_key, 1)
                n += 1
                dve.wait_ge(s_key, n)
            dve.tensor_copy(rank[:, :], rank_f[:, :]).then_inc(s_rank, 1)

            dve.wait_ge(s_weights, 16 * 20)
            dve.tensor_tensor(w_keys[E:P, :], w_keys[E:P, :], w_diff_hi[E:P, :], ALU.subtract).then_inc(s_wprep, 1)
            dve.tensor_tensor(w_q[0:E, :], w_q[0:E, :], w_diff_lo[:, :], ALU.add).then_inc(s_wprep, 1)
            dve.tensor_scalar(coslopes[:, :], slopes[:, :], -1.0, 1.0, ALU.mult, ALU.add).then_inc(s_wprep, 1)

            dve.wait_ge(s_lead, 16)
            dve.tensor_scalar(lead_full[:, :], lead[:, :], 0.0, float(T), ALU.is_le, ALU.mult).then_inc(s_plan, 1)
            dve.tensor_scalar(lead_f[:, :], lead[:, :], 0.0, float(T), ALU.max, ALU.min).then_inc(s_plan, 1)
            dve.wait_ge(s_plan, 2)
            dve.tensor_tensor(lead_f[:, :], lead_f[:, :], lead_full[:, :], ALU.add).then_inc(s_plan, 1)
            dve.wait_ge(s_plan, 3)
            dve.tensor_tensor(pass_used[:, :, :], lead_f[:, :].unsqueeze(2).broadcast_to([1, GROUPS, PASSES]),
                              pass_start[:, :].unsqueeze(1).broadcast_to([1, GROUPS, PASSES]), ALU.is_gt) \
                .then_inc(s_plan, 1)
            dve.wait_ge(s_plan, 4)
            dve.tensor_reduce(n_pass[:, :], pass_used[:, :, :], AX_X, ALU.add).then_inc(s_plan, 1)
            dve.wait_ge(s_plan, 5)
            dve.tensor_scalar(n_pass[:, :], n_pass[:, :], 2.0, None, ALU.max).then_inc(s_plan, 1)
            dve.memset(first_pass[:, 0:1], 0).then_inc(s_plan, 1)
            dve.wait_ge(s_plan, 7)
            dve.tensor_tensor_scan(pass_end[:, :], n_pass[:, :], zeros16[:, :], 0.0, ALU.add, ALU.add) \
                .then_inc(s_plan, 1)
            dve.wait_ge(s_plan, 8)
            dve.tensor_copy(first_pass[:, 1:GROUPS + 1], pass_end[:, :]).then_inc(s_planned, 1)

            for n, ahead in enumerate((s_head_used, s_group, s_sum[1], *s_summed)):
                dve.memset(spare[:, n:n + 1], 0.0).then_inc(ahead, 1)

            def fill(k, i):
                rows_ = keys[k][:, 0:CHUNK, :]
                dve.wait_ge(s_got[k], (i + 1) * (16 * 2 * CHUNK))
                dve.tensor_tensor(rows_[:, :, E:P], got[k][:, 0, :, :], got[k][:, 1, :, :], ALU.add) \
                    .then_inc(s_summed[k], 1)
                dve.wait_ge(s_summed[k], i + 2)
                dve.tensor_tensor(rows_[:, :, 0:E], rows_[:, :, E:P],
                                  q_cur[:, :].unsqueeze(1).broadcast_to([P, CHUNK, E]), ALU.mult) \
                    .then_inc(s_keys[k], 1)

            def prelu(hid, neg, x, coslope, done):
                dve.scalar_tensor_tensor(hid, neg, coslope, x, ALU.mult, ALU.add).then_inc(done, 1)

            def prelu0(k, i):
                dve.wait_ge(s_neg0[k], i + 1)
                prelu(hid_0[k][0:H0, :], neg_0[k][:, :], p_0[k][0:H0, :], coslopes[0:H0, 0:1], s_hid0[k])

            def prelu1(k, i):
                dve.wait_ge(s_neg1[k], i + 1)
                prelu(hid_1[k][0:H1, :], neg_1[k][:, :], p_1[k][0:H1, :], coslopes[0:H1, 1:2], s_hid1[k])

            def scores(k, i):
                o = 1 - k
                dve.tensor_scalar(open_[k][:, :], place[k][:, :], left[:, 0:1], HUGE, ALU.is_lt, ALU.mult) \
                    .then_inc(s_open[k], 1)
                dve.wait_ge(s_l2[k], i + 1)
                dve.wait_ge(s_open[k], i + 1)
                dve.scalar_tensor_tensor(score[k][:, 0:CHUNK], open_[k][:, :], MASKED,
                                         p_s[:, k * CHUNK:(k + 1) * CHUNK], ALU.add, ALU.min) \
                    .then_inc(s_masked[k], 1)
                if k == SLOTS - 1:
                    dve.tensor_scalar(left[:, :], left[:, :], -float(PASS), None, ALU.add).then_inc(s_left, 1)
                dve.wait_ge(s_masked[k], i + 1)
                dve.tensor_reduce(score[o][:, CHUNK:CHUNK + 1], score[k][:, :], AX_X, ALU.max) \
                    .then_inc(s_max[k], 1)
                dve.wait_ge(s_max[k], i + 1)
                dve.tensor_scalar(below[k][:, :], score[k][:, :], score[o][:, CHUNK:CHUNK + 1], None,
                                  ALU.subtract).then_inc(s_below[k], 1)

            def weigh(k, i):
                o = 1 - k
                dve.wait_ge(s_prob[k], i + 1)
                dve.wait_ge(s_sum[o], i + 1)
                if k == SLOTS - 1:
                    dve.wait_ge(s_left, i + 1)
                dve.tensor_tensor(part[k][:, :, :], keys[k][:, :, E:P + 1],
                                  prob[k][:, :].unsqueeze(2).broadcast_to([P, CHUNK + 1, W]), ALU.mult) \
                    .then_inc(s_part[k], 1)
                dve.wait_ge(s_part[k], i + 1)
                dve.tensor_reduce(keys[o][:, CHUNK, E:P + 1], part[k][:, :, :].rearrange("p t e -> p e t"),
                                  AX_X, ALU.add).then_inc(s_sum[k], 1)

            def step(k, i, before):
                fill(k, i)
                if before:
                    prelu1(*before)
                    scores(*before)
                prelu0(k, i)
                if before:
                    weigh(*before)

            dve.wait_ge(s_planned, 1)
            with dve.Fori(0, GROUPS) as g:
                first, end = passes(dve, g)
                dve.wait_ge(s_head_idx, (g + 1) * 16)
                dve.wait_ge(s_head, (g + 1) * (16 * 3))
                dve.tensor_copy(q_cur[:, :], head[:, 1, :]).then_inc(s_q_cur, 1)
                dve.tensor_copy(left[:, :], head_idx[:, 0:1]).then_inc(s_state, 1)
                dve.memset(score[0][:, CHUNK:CHUNK + 1], -HUGE).then_inc(s_state, 1)
                dve.wait_ge(s_group, g + 1)
                dve.memset(keys[0][:, CHUNK, E:P + 1], 0.0).then_inc(s_state, 1)
                dve.tensor_copy(feat[:, bass.ds(g, 1), 0:3 * E].rearrange("p a b -> p (a b)"),
                                head[:, :, :].rearrange("p a b -> p (a b)")).then_inc(s_head_used, 1)
                dve.wait_ge(s_q_cur, g + 1)
                dve.wait_ge(s_state, (g + 1) * 3)
                step(0, first, None)
                step(1, first, (0, first))
                with dve.Fori(first + 1, end) as i:
                    step(0, i, (1, i - 1))
                    step(1, i, (0, i))
                prelu1(1, end - 1)
                scores(1, end - 1)
                weigh(1, end - 1)
                dve.wait_ge(s_sum[1], end + 1)
                dve.reciprocal(inv_sum[:, :], keys[0][:, CHUNK, P:P + 1]).then_inc(s_inv, 1)
                dve.wait_ge(s_inv, g + 1)
                dve.tensor_scalar(feat[:, bass.ds(g, 1), 3 * E:4 * E].rearrange("p a b -> p (a b)"),
                                  keys[0][:, CHUNK, E:P], inv_sum[:, 0:1], None, ALU.mult).then_inc(s_group, 1)

            n_pe = n_act = n_dve = 0
            for b in range(B // COLS):
                n_pe += 2
                n_act += 2
                for x, xs, neg, hid, bias, cos in (
                        (p_0[0][0:M0, :], mx_0, mneg_0, mhid_0, mb_0, coslopes[0:M0, 2:3]),
                        (p_1[0][0:M1, :], mx_1, mneg_1, mhid_1, mb_1, coslopes[0:M1, 3:4])):
                    n_pe += 1
                    n_act += 1
                    dve.wait_ge(s_mlp_pe, n_pe)
                    dve.tensor_scalar(xs[:, :], x, bias[:, 0:1], None, ALU.add).then_inc(s_mlp_dve, 1)
                    n_dve += 1
                    dve.wait_ge(s_mlp_dve, n_dve)
                    dve.wait_ge(s_mlp_act, n_act)
                    prelu(hid[0:xs.shape[0], :], neg[:, :], xs[:, :], cos, s_mlp_dve)
                    n_dve += 1
                n_pe += 1


def kernel(**inputs):
    import numpy as np
    import concourse.bacc as bacc
    from concourse.bass_utils import run_bass_kernel_spmd as run

    x = {name: np.asarray(a) for name, a in inputs.items()}
    tags, artists = x["r_hist_tags"], x["r_hist_artists"]
    B, T = tags.shape
    hist = np.stack([tags.reshape(B, T // CHUNK, CHUNK), artists.reshape(B, T // CHUNK, CHUNK)], axis=2)
    own = np.stack([x["r_seq_lengths"], x["r_user_id"], x["r_target_tag"], x["r_target_artist"],
                    np.arange(B, dtype=np.int32)] + [np.zeros(B, np.int32)] * (META - 5), axis=1)
    arrays = {
        "lengths": x["r_seq_lengths"],
        "rows": np.concatenate([hist.reshape(B, 2 * T), own], axis=1),
        "user_table": x["L0_rec_user_table"], "tag_table": x["L0_rec_tag_table"],
        "artist_table": x["L0_rec_artist_table"],
    }
    for net in ("att", "mlp"):
        for n in range(3):
            arrays[f"{net}_w{n}"] = x[f"L0_rec_{net}_w{n}"].T
            arrays[f"{net}_b{n}"] = x[f"L0_rec_{net}_b{n}"]
            arrays[f"{net}_b{n}"] = arrays[f"{net}_b{n}"][:, None] if net == "mlp" and n < 2 \
                else arrays[f"{net}_b{n}"][None, :]
            if n < 2:
                arrays[f"{net}_a{n}"] = x[f"L0_rec_{net}_a{n}"]
    nc = bacc.Bacc("TRN2", target_bir_lowering=False, num_devices=1)
    arrays = {name: np.ascontiguousarray(a) for name, a in arrays.items()}
    t = {name: nc.dram_tensor(name, a.shape, mybir.dt.from_np(a.dtype), kind="ExternalInput").ap()
         for name, a in arrays.items()}
    sorted_rows = nc.dram_tensor("sorted_rows", arrays["rows"].shape, I32, kind="Internal").ap()
    out = nc.dram_tensor("out", (B, 1), F32, kind="ExternalOutput").ap()
    net = [t[f"{n}_{p}"] for n in ("att", "mlp") for p in ("w0", "b0", "a0", "w1", "b1", "a1", "w2", "b2")]
    program(nc, t["lengths"], t["rows"], t["user_table"], t["tag_table"], t["artist_table"], *net, sorted_rows, out)
    return run(nc, [arrays], core_ids=[0]).results[0]["out"].reshape(B)
```

```python
from contextlib import ExitStack

import concourse.bass as bass
from concourse import mybir

F32 = mybir.dt.float32
I32 = mybir.dt.int32
U32 = mybir.dt.uint32
ALU = mybir.AluOpType
ACT = mybir.ActivationFunctionType
AX_X = mybir.AxisListType.X

P = 128
CHUNK = 4
SLOTS = 2
PASS = CHUNK * SLOTS
MASKED = -1000000000.0
HUGE = 3.0e38
META = 8


def program(nc, lengths, rows, user_table, tag_table, artist_table, a_w0, a_b0, a_a0, a_w1, a_b1, a_a1,
            a_w2, a_b2, m_w0, m_b0, m_a0, m_w1, m_b1, m_a1, m_w2, m_b2, keys_dram, sorted_rows, out):
    B, ROW = rows.shape
    T = ROW - META
    N, E = tag_table.shape
    GROUPS = B // P
    H0, H1 = a_w0.shape[1], a_w1.shape[1]
    M0, M1 = m_w0.shape[1], m_w1.shape[1]
    T //= 2
    PASSES = T // PASS
    COLS = CHUNK * P
    X0, X1 = H0 + 1, H1 + 1
    HALF_P = P // 2
    PAIRS = COLS // 2
    W = E + 1
    assert user_table.shape[0] == N and artist_table.shape[0] == N
    assert 2 * E == P and T % PASS == 0 and X0 <= P and X1 <= HALF_P and CHUNK == 4

    with ExitStack() as ctx:
        def sb(name, shape, dt=F32):
            return ctx.enter_context(nc.sbuf_tensor(name, shape, dt))

        def ps(name, shape):
            return ctx.enter_context(nc.psum_tensor(name, shape, F32))

        def sem(name):
            return ctx.enter_context(nc.semaphore(name))

        def sems(name):
            return [sem(f"{name}{k}") for k in range(SLOTS)]

        len_own = sb("len_own", [P, GROUPS], I32)
        tie_own = sb("tie_own", [P, GROUPS])
        full_own = sb("full_own", [P, GROUPS])
        walk_own = sb("walk_own", [P, GROUPS])
        key_own = sb("key_own", [P, GROUPS])
        neg_key = sb("neg_key", [P, GROUPS])
        key_row = sb("key_row", [P, B])
        beats = sb("beats", [P, B])
        signs = sb("signs", [P, B])
        sign_sum = sb("sign_sum", [P, GROUPS])
        rank_f = sb("rank_f", [P, GROUPS])
        rank = sb("rank", [P, GROUPS], U32)
        row_sb = sb("row_sb", [P, GROUPS, ROW], I32)
        wrap = sb("wrap", [P, GROUPS, ROW], I32)
        perm = sb("perm", [P, GROUPS], I32)
        pass_start = sb("pass_start", [P, PASSES])
        walks = sb("walks", [P, PASSES, GROUPS])
        walk_sum = sb("walk_sum", [P, PASSES])
        ones = sb("ones", [P, 1])
        group_start = sb("group_start", [1, GROUPS])
        users_in = sb("users_in", [1, PASSES])
        pass_used = sb("pass_used", [1, GROUPS, PASSES])
        n_pass = sb("n_pass", [1, GROUPS])
        zeros16 = sb("zeros16", [1, GROUPS])
        spare = sb("spare", [1, 8])
        pass_end = sb("pass_end", [1, GROUPS])
        first_pass = sb("first_pass", [1, GROUPS + 1], I32)

        ident = sb("ident", [P, P])
        w_keys = sb("w_keys", [P, X0])
        w_diff_hi = sb("w_diff_hi", [P, H0])
        w_q = sb("w_q", [E + 1, X0])
        w_diff_lo = sb("w_diff_lo", [E, H0])
        w_1 = sb("w_1", [X0, HALF_P])
        w_2 = sb("w_2", [P, 2])
        slopes = sb("slopes", [P, 4])
        coslopes = sb("coslopes", [P, 4])
        mw_0 = sb("mw_0", [P, 2, M0])
        mb_0 = sb("mb_0", [M0, 1])
        mw_1 = sb("mw_1", [M0, M1])
        mb_1 = sb("mb_1", [M1, 1])
        mw_2 = sb("mw_2", [M1 + 1, 1])

        head_idx = sb("head_idx", [P, META], I32)
        head = sb("head", [P, 3, E])
        q_cur = sb("q_cur", [P, E])
        q_t = sb("q_t", [E + 1, P])
        left = sb("left", [P, 1])
        inv_sum = sb("inv_sum", [P, 1])
        feat = sb("feat", [P, GROUPS, 4 * E])

        stage = [sb(f"stage{k}", [P, 2 * CHUNK], I32) for k in range(SLOTS)]
        got = [sb(f"got{k}", [P, 2, CHUNK, E]) for k in range(SLOTS)]
        keys = [sb(f"keys{k}", [P, CHUNK + 1, P + 1]) for k in range(SLOTS)]
        keys_t = [sb(f"keys_t{k}", [P, COLS]) for k in range(SLOTS)]
        neg_0 = [sb(f"neg_0{k}", [X0, COLS]) for k in range(SLOTS)]
        hid_0 = [sb(f"hid_0{k}", [X0, COLS]) for k in range(SLOTS)]
        neg_1 = [sb(f"neg_1{k}", [P, PAIRS]) for k in range(SLOTS)]
        hid_1 = [sb(f"hid_1{k}", [P, PAIRS]) for k in range(SLOTS)]
        place = [sb(f"place{k}", [P, CHUNK]) for k in range(SLOTS)]
        open_ = [sb(f"open{k}", [P, CHUNK]) for k in range(SLOTS)]
        score = [sb(f"score{k}", [P, CHUNK + 1]) for k in range(SLOTS)]
        below = [sb(f"below{k}", [P, CHUNK + 1]) for k in range(SLOTS)]
        prob = [sb(f"prob{k}", [P, CHUNK + 1]) for k in range(SLOTS)]
        part = [sb(f"part{k}", [P, CHUNK + 1, W]) for k in range(SLOTS)]

        feat_t = [sb(f"feat_t{k}", [P, 2, COLS]) for k in range(2)]
        mx_0 = [sb(f"mx_0{k}", [M0, COLS]) for k in range(2)]
        mneg_0 = [sb(f"mneg_0{k}", [M0, COLS]) for k in range(2)]
        mhid_0 = [sb(f"mhid_0{k}", [M0, COLS]) for k in range(2)]
        mx_1 = [sb(f"mx_1{k}", [M1, COLS]) for k in range(2)]
        mneg_1 = [sb(f"mneg_1{k}", [M1, COLS]) for k in range(2)]
        mhid_1 = [sb(f"mhid_1{k}", [M1 + 1, COLS]) for k in range(2)]
        result = sb("result", [P, GROUPS])

        p_t = [ps(f"p_t{k}", [P, COLS]) for k in range(SLOTS)]
        p_0 = [ps(f"p_0{k}", [P, COLS]) for k in range(SLOTS)]
        p_1 = [ps(f"p_1{k}", [P, COLS]) for k in range(SLOTS)]
        p_s = ps("p_s", [P, COLS])
        p_q = ps("p_q", [P, COLS])
        p_m = [p_s, p_q, *p_t]

        s_len = sem("s_len")
        s_rows = sem("s_rows")
        s_const = sem("s_const")
        s_key = sem("s_key")
        s_own_keys = sem("s_own_keys")
        s_key_out = sem("s_key_out")
        s_key_row = sem("s_key_row")
        s_walk_sum = sem("s_walk_sum")
        s_users_in = sem("s_users_in")
        s_beats = sem("s_beats")
        s_signs = sem("s_signs")
        s_rank = sem("s_rank")
        s_wrap = sem("s_wrap")
        s_clamped = sem("s_clamped")
        s_scattered = sem("s_scattered")
        s_plan = sem("s_plan")
        s_planned = sem("s_planned")
        s_perm = sem("s_perm")
        s_zeroed = sem("s_zeroed")
        s_weights = sem("s_weights")
        s_wprep = sem("s_wprep")
        s_ones = sem("s_ones")

        s_head_idx = sem("s_head_idx")
        s_head = sem("s_head")
        s_taken = sem("s_taken")
        s_head_used = sem("s_head_used")
        s_q_cur = sem("s_q_cur")
        s_q_turned = sem("s_q_turned")
        s_q_t = sem("s_q_t")
        s_state = sem("s_state")
        s_left = sem("s_left")
        s_inv = sem("s_inv")
        s_group = sem("s_group")

        s_stage = sems("s_stage")
        s_got = sems("s_got")
        s_summed = sems("s_summed")
        s_keys = sems("s_keys")
        s_turned = sems("s_turned")
        s_keys_t = sems("s_keys_t")
        s_l0 = sems("s_l0")
        s_neg0 = sems("s_neg0")
        s_hid0 = sems("s_hid0")
        s_l1 = sems("s_l1")
        s_neg1 = sems("s_neg1")
        s_hid1 = sems("s_hid1")
        s_l2 = sems("s_l2")
        s_open = sems("s_open")
        s_masked = sems("s_masked")
        s_max = sems("s_max")
        s_below = sems("s_below")
        s_prob = sems("s_prob")
        s_part = sems("s_part")
        s_sum = sems("s_sum")

        s_feat_t = sem("s_feat_t")
        s_feat_sb = sem("s_feat_sb")
        s_m0 = sem("s_m0")
        s_mx0 = sem("s_mx0")
        s_mneg0 = sem("s_mneg0")
        s_mhid0 = sem("s_mhid0")
        s_m1 = sem("s_m1")
        s_mx1 = sem("s_mx1")
        s_mneg1 = sem("s_mneg1")
        s_mhid1 = sem("s_mhid1")
        s_m2 = sem("s_m2")
        s_result = sem("s_result")
        s_out = sem("s_out")

        BATCHES = B // COLS
        assert BATCHES == len(p_m)
        HALF = GROUPS // 2

        CLAMPS = [(0, GROUPS, 2 * T + 1, 2 * T + 4), (0, HALF, 0, 2 * T), (HALF, GROUPS, 0, 2 * T)]

        block = ctx.enter_context(nc.Block())

        def passes(eng, g):
            a = eng.value_load(first_pass[0:1, bass.ds(g, 1)], min_val=0, max_val=GROUPS * PASSES)
            b = eng.value_load(first_pass[0:1, bass.ds(g + 1, 1)], min_val=0, max_val=GROUPS * PASSES)
            return a, b

        def first_end(eng):
            return eng.value_load(first_pass[0:1, 1:2], min_val=2, max_val=PASSES)

        @block.sync
        def _(sp):
            sp.dma_start(len_own[:, :], lengths.rearrange("(p j) -> p j", p=P)).then_inc(s_len, 16)
            sp.dma_start(row_sb[:, :, :], rows.rearrange("(p j) c -> p j c", p=P)).then_inc(s_rows, 16)
            sp.wait_ge(s_own_keys, 1)
            sp.dma_start(keys_dram.rearrange("(p j) -> p j", p=P), key_own[:, :]).then_inc(s_key_out, 16)
            sp.wait_ge(s_key_out, 16)
            sp.dma_start(key_row[:, :], keys_dram.partition_broadcast(P)).then_inc(s_key_row, 16)

            sp.wait_ge(s_scattered, 16 * GROUPS)
            sp.wait_ge(s_planned, 1)

            heads, landed = (sp.alloc_register(name) for name in ("heads", "landed"))
            sp.reg_mov(heads, 0)
            sp.reg_mov(landed, 0)

            def load_head(g, again):
                sp.reg_add(heads, heads, 1)
                sp.wait_ge(s_planned, 1)
                sp.wait_ge(s_head_used, heads)
                if again:
                    sp.wait_ge(s_got[0], landed)
                sp.dma_start(head_idx[:, :], sorted_rows[bass.ds(g * P, P), 2 * T:2 * T + META]) \
                    .then_inc(s_head_idx, 16)

            def load_stage(g, col, waits):
                for k in range(SLOTS):
                    if k in waits:
                        sp.wait_ge(s_planned, 1)
                        sp.wait_ge(s_got[k], landed)
                    sp.dma_start(stage[k][:, :],
                                 sorted_rows[bass.ds(g * P, P), bass.ds(col + 2 * CHUNK * k, 2 * CHUNK)]) \
                        .then_inc(s_stage[k], 16)
                sp.reg_add(landed, landed, 16 * 2 * CHUNK)

            def group(g, first, end):
                again = not isinstance(first, int)
                load_head(g, again)
                load_stage(g, 0, range(1, SLOTS) if again else ())
                with sp.Fori(first + 1, end) as i:
                    load_stage(g, nc.s_assert_within((i - first) * (2 * PASS), 2 * PASS, (PASSES - 1) * (2 * PASS),
                               skip_runtime_bounds_check_because="a group has at most PASSES passes"),
                               range(SLOTS))

            group(0, 0, first_end(sp))
            with nc.allow_non_contiguous_dma(reason="one word per user, once"):
                sp.dma_start(perm[:, :], sorted_rows.rearrange("(g p) c -> p g c", p=P)[:, :, 2 * T + 4]) \
                    .then_inc(s_perm, 16)
            with sp.Fori(1, GROUPS) as g:
                group(g, *passes(sp, g))

        @block.gpsimd
        def _(pool):
            pool.iota(tie_own[:, :], [[-1, GROUPS]], base=B - 1, channel_multiplier=-GROUPS,
                      allow_small_or_imprecise_dtypes=True).then_inc(s_const, 1)
            pool.iota(pass_start[:, :], [[PASS, PASSES]], base=0, channel_multiplier=0,
                      allow_small_or_imprecise_dtypes=True).then_inc(s_const, 1)
            pool.iota(group_start[:, :], [[P, GROUPS]], base=0, channel_multiplier=0,
                      allow_small_or_imprecise_dtypes=True).then_inc(s_const, 1)
            for k in range(SLOTS):
                pool.iota(place[k][:, :], [[1, CHUNK]], base=CHUNK * k, channel_multiplier=0,
                          allow_small_or_imprecise_dtypes=True).then_inc(s_const, 1)
            pool.memset(ident[:, :], 0.0).then_inc(s_const, 1)
            pool.wait_ge(s_const, 6)
            pool.affine_select(out=ident[:, :], in_=ident[:, :], compare_op=ALU.not_equal, fill=1.0,
                               base=0, pattern=[[-1, P]], channel_multiplier=1).then_inc(s_const, 1)
            pool.wait_ge(s_rank, 1)
            pool.wait_ge(s_clamped, 3)
            for j in range(GROUPS):
                pool.indirect_dma_start(
                    out=sorted_rows, out_offset=bass.IndirectOffsetOnAxis(ap=rank[:, j:j + 1], axis=0),
                    in_=row_sb[:, j, :], in_offset=None).then_inc(s_scattered, 16)

            head_loads, turn, loads = (pool.alloc_register(name) for name in ("head_loads", "turn", "loads"))
            for register in (head_loads, turn, loads):
                pool.reg_mov(register, 0)
            pool.wait_ge(s_planned, 1)
            with pool.Fori(0, GROUPS) as g:
                first, end = passes(pool, g)
                pool.reg_add(head_loads, head_loads, 16)
                pool.wait_ge(s_planned, 1)
                pool.wait_ge(s_head_idx, head_loads)
                for n, (table, col) in enumerate(((user_table, 1), (tag_table, 2), (artist_table, 3))):
                    pool.indirect_dma_start(
                        out=head[:, n, :], out_offset=None, in_=table,
                        in_offset=bass.IndirectOffsetOnAxis(ap=head_idx[:, col:col + 1].bitcast(U32), axis=0)) \
                        .then_inc(s_head, 16)
                with pool.Fori(first, end) as i:
                    pool.reg_add(turn, turn, 1)
                    pool.reg_add(loads, loads, 16)
                    for k in range(SLOTS):
                        pool.wait_ge(s_planned, 1)
                        pool.wait_ge(s_stage[k], loads)
                        pool.wait_ge(s_summed[k], turn)
                        for n, table in enumerate((tag_table, artist_table)):
                            for t in range(CHUNK):
                                c = n * CHUNK + t
                                pool.indirect_dma_start(
                                    out=got[k][:, n, t, :], out_offset=None, in_=table,
                                    in_offset=bass.IndirectOffsetOnAxis(
                                        ap=stage[k][:, c:c + 1].bitcast(U32), axis=0)).then_inc(s_got[k], 16)
            pool.wait_ge(s_perm, 16)
            for g in range(GROUPS):
                if g % CHUNK == 0:
                    pool.wait_ge(s_result, g // CHUNK + 1)
                pool.indirect_dma_start(
                    out=out, out_offset=bass.IndirectOffsetOnAxis(ap=perm[:, g:g + 1].bitcast(U32), axis=0),
                    in_=result[:, g:g + 1], in_offset=None).then_inc(s_out, 16)
            pool.wait_ge(s_out, 16 * GROUPS)

        @block.scalar
        def _(act):
            act.wait_ge(s_zeroed, 1)
            act.wait_ge(s_ones, 1)
            loads = [
                (w_keys[0:E, 0:H0], a_w0[3 * E:4 * E, :]), (w_keys[E:P, 0:H0], a_w0[E:2 * E, :]),
                (w_diff_hi[E:P, :], a_w0[2 * E:3 * E, :]), (w_diff_lo[:, :], a_w0[2 * E:3 * E, :]),
                (w_q[0:E, 0:H0], a_w0[0:E, :]), (w_q[E:E + 1, 0:H0], a_b0),
                (w_1[0:H0, 0:H1], a_w1), (w_1[H0:X0, 0:H1], a_b1), (w_1[H0:X0, H1:X1], ones[0:1, 0:1]),
                (w_2[0:H1, 0:1], a_w2), (w_2[H1:X1, 0:1], a_b2),
                (w_2[HALF_P:HALF_P + H1, 1:2], a_w2), (w_2[HALF_P + H1:HALF_P + X1, 1:2], a_b2),
                (mw_0[:, :, :], m_w0.rearrange("(h k) n -> k h n", h=2)), (mw_1[:, :], m_w1),
                (mw_2[0:M1, :], m_w2), (mw_2[M1:M1 + 1, :], m_b2),
                (mb_0[:, :], m_b0), (mb_1[:, :], m_b1),
            ]
            for dst, src in loads:
                act.dma_start(dst, src).then_inc(s_weights, 16)
            for n, a in enumerate((a_a0, a_a1, m_a0, m_a1)):
                act.dma_start(slopes[:, n:n + 1], a.partition_broadcast(P)).then_inc(s_weights, 16)

            act.wait_ge(s_key_row, 16)
            act.wait_ge(s_own_keys, 2)
            for j in range(HALF, GROUPS):
                if j > HALF:
                    act.wait_ge(s_signs, j - HALF)
                act.activation(signs[:, :], key_row[:, :], ACT.Sign, bias=neg_key[:, j:j + 1],
                               accum_out=sign_sum[:, j:j + 1]).then_inc(s_signs, 1)
            for n, (j0, j1, lo, hi) in enumerate(CLAMPS):
                act.wait_ge(s_wrap, 2 * n + 2)
                act.activation(row_sb[:, j0:j1, lo:hi], row_sb[:, j0:j1, lo:hi], ACT.Relu).then_inc(s_clamped, 1)

            def turn(k, i):
                act.wait_ge(s_turned[k], i + 1)
                act.activation(keys_t[k][:, :], p_t[k][:, :], ACT.Copy).then_inc(s_keys_t[k], 1)

            def relu0(k, i):
                act.wait_ge(s_l0[k], i + 1)
                act.activation(neg_0[k][:, :], p_0[k][0:X0, :], ACT.Relu, scale=-1.0).then_inc(s_neg0[k], 1)

            def relu1(k, i):
                act.wait_ge(s_l1[k], i + 1)
                act.activation(neg_1[k][:, :], p_1[k][:, 0:PAIRS], ACT.Relu, scale=-1.0).then_inc(s_neg1[k], 1)

            def exp(k, i):
                act.wait_ge(s_below[k], i + 1)
                act.activation(prob[k][:, :], below[k][:, :], ACT.Exp).then_inc(s_prob[k], 1)

            def step(k, i, before):
                relu1(*before)
                turn(k, i)
                relu0(k, i)
                exp(*before)

            def group(g, first, end, before):
                if before:
                    relu1(*before)
                act.wait_ge(s_q_turned, g + 1)
                act.activation(q_t[0:E, :], p_q[0:E, 0:P], ACT.Copy).then_inc(s_q_t, 1)
                turn(0, first)
                relu0(0, first)
                if before:
                    exp(*before)
                step(1, first, (0, first))
                with act.Fori(first + 1, end) as i:
                    step(0, i, (1, i - 1))
                    step(1, i, (0, i))

            act.wait_ge(s_planned, 1)
            group(0, 0, first_end(act), None)
            with act.Fori(1, GROUPS) as g:
                first, end = passes(act, g)
                group(g, first, end, (1, first - 1))
            end = act.value_load(first_pass[0:1, GROUPS:GROUPS + 1], min_val=2, max_val=GROUPS * PASSES)
            relu1(1, end - 1)
            exp(1, end - 1)

            def features(b):
                for h in range(2):
                    act.wait_ge(s_feat_t, 2 * b + h + 1)
                    act.activation(feat_t[b % 2][:, h, :], p_t[h][:, :], ACT.Copy).then_inc(s_feat_sb, 1)

            for b in range(BATCHES):
                if b == 0:
                    features(b)
                act.wait_ge(s_mx0, b + 1)
                act.activation(mneg_0[b % 2][:, :], mx_0[b % 2][:, :], ACT.Relu, scale=-1.0).then_inc(s_mneg0, 1)
                if b + 1 < BATCHES:
                    features(b + 1)
                act.wait_ge(s_mx1, b + 1)
                act.activation(mneg_1[b % 2][:, :], mx_1[b % 2][:, :], ACT.Relu, scale=-1.0).then_inc(s_mneg1, 1)
            for b in range(BATCHES):
                act.wait_ge(s_m2, b + 1)
                act.activation(result[:, b * CHUNK:(b + 1) * CHUNK], p_m[b][:, 0:CHUNK], ACT.Sigmoid) \
                    .then_inc(s_result, 1)

        @block.tensor
        def _(pe):
            pe.wait_ge(s_walk_sum, 1)
            pe.matmul(p_q[0:1, 0:PASSES], ones[:, :], walk_sum[:, :], start=True, stop=True).then_inc(s_users_in, 1)
            pe.wait_ge(s_const, 7)
            pe.wait_ge(s_wprep, 2)
            pe.wait_ge(s_ones, 1)

            def turn(k, i):
                pe.wait_ge(s_keys[k], i + 1)
                for t in range(CHUNK):
                    mm = pe.transpose(p_t[k][:, t * P:(t + 1) * P], keys[k][:, t, 0:P], ident[:, :])
                mm.then_inc(s_turned[k], 1)

            def target(k):
                pe.matmul(p_0[k][0:X0, :], w_q[:, :], q_t[:, :].unsqueeze(1).broadcast_to([E + 1, CHUNK, P]),
                          start=True, stop=False)

            def layer0(k, i):
                pe.wait_ge(s_keys_t[k], i + 1)
                pe.matmul(p_0[k][0:X0, :], w_keys[:, :], keys_t[k][:, :],
                          start=False, stop=True).then_inc(s_l0[k], 1)

            def layer1(k, i):
                by_parity = hid_0[k][:, :].rearrange("h (t s b) -> h s t b", s=2, b=P)
                pe.wait_ge(s_hid0[k], i + 1)
                for s in range(2):
                    mm = pe.matmul(p_1[k][s * HALF_P:(s + 1) * HALF_P, 0:PAIRS], w_1[:, :], by_parity[:, s],
                                   start=True, stop=True)
                mm.then_inc(s_l1[k], 1)

            def layer2(k, i):
                pe.wait_ge(s_hid1[k], i + 1)
                for t in range(0, CHUNK, 2):
                    c = k * CHUNK + t
                    mm = pe.matmul(p_s[:, c:c + 2], hid_1[k][:, t * P // 2:(t + 2) * P // 2], w_2[:, :],
                                   start=True, stop=True)
                mm.then_inc(s_l2[k], 1)

            def step(k, i, before):
                target(k)
                turn(k, i)
                layer0(k, i)
                layer2(*before)
                layer1(k, i)

            def group(g, first, end, before):
                pe.wait_ge(s_planned, 1)
                pe.wait_ge(s_q_cur, g + 1)
                pe.transpose(p_q[0:E, 0:P], q_cur[:, :], ident[:, :]).then_inc(s_q_turned, 1)
                turn(0, first)
                pe.wait_ge(s_q_t, g + 1)
                target(0)
                layer0(0, first)
                if before:
                    layer2(*before)
                layer1(0, first)
                step(1, first, (0, first))
                with pe.Fori(first + 1, end) as i:
                    step(0, i, (1, i - 1))
                    step(1, i, (0, i))

            pe.wait_ge(s_planned, 1)
            group(0, 0, first_end(pe), None)
            with pe.Fori(1, GROUPS) as g:
                first, end = passes(pe, g)
                group(g, first, end, (1, first - 1))
            end = pe.value_load(first_pass[0:1, GROUPS:GROUPS + 1], min_val=2, max_val=GROUPS * PASSES)
            layer2(1, end - 1)

            def features(b):
                if b:
                    pe.wait_ge(s_feat_sb, 2 * b)
                for h in range(2):
                    for g in range(CHUNK):
                        mm = pe.transpose(p_t[h][:, g * P:(g + 1) * P],
                                          feat[:, b * CHUNK + g, h * P:(h + 1) * P], ident[:, :])
                    mm.then_inc(s_feat_t, 1)

            pe.wait_ge(s_group, GROUPS)
            features(0)
            for b in range(BATCHES):
                pe.wait_ge(s_feat_sb, 2 * b + 2)
                for h in range(2):
                    mm = pe.matmul(p_0[b % 2][0:M0, :], mw_0[:, h, :], feat_t[b % 2][:, h, :],
                                   start=h == 0, stop=h == 1)
                mm.then_inc(s_m0, 1)
                if b + 1 < BATCHES:
                    if b + 2 == BATCHES:
                        pe.wait_ge(s_group, GROUPS + 1)
                    features(b + 1)
                pe.wait_ge(s_mhid0, b + 1)
                pe.matmul(p_1[b % 2][0:M1, :], mw_1[:, :], mhid_0[b % 2][:, :], start=True, stop=True) \
                    .then_inc(s_m1, 1)
                pe.wait_ge(s_mhid1, b + 1)
                for g in range(CHUNK):
                    mm = pe.matmul(p_m[b][:, g:g + 1], mhid_1[b % 2][:, g * P:(g + 1) * P], mw_2[:, :],
                                   start=True, stop=True)
                mm.then_inc(s_m2, 1)

        @block.vector
        def _(dve):
            for tile in (w_keys, w_q, w_1, w_2):
                ins = dve.memset(tile[:, :], 0.0)
            ins.then_inc(s_zeroed, 1)
            dve.wait_ge(s_zeroed, 1)
            dve.memset(w_q[E:E + 1, H0:X0], 1.0)
            for tile, row in ((q_t, E), (mhid_1[0], M1), (mhid_1[1], M1)):
                dve.memset(tile[row:row + 1, :], 1.0)
            for k in range(SLOTS):
                dve.memset(keys[k][:, :, P:P + 1], 1.0)
            dve.memset(ones[:, :], 1.0)
            dve.memset(zeros16[:, :], 0.0).then_inc(s_ones, 1)

            dve.wait_ge(s_len, 16)
            dve.wait_ge(s_const, 3)
            dve.tensor_scalar(full_own[:, :], len_own[:, :], 0.0, float(T), ALU.is_le, ALU.mult).then_inc(s_key, 1)
            dve.tensor_scalar(walk_own[:, :], len_own[:, :], 0.0, float(T), ALU.max, ALU.min).then_inc(s_key, 1)
            dve.wait_ge(s_key, 2)
            dve.tensor_tensor(walk_own[:, :], full_own[:, :], walk_own[:, :], ALU.add).then_inc(s_key, 1)
            dve.wait_ge(s_key, 3)
            dve.scalar_tensor_tensor(key_own[:, :], walk_own[:, :], float(B), tie_own[:, :], ALU.mult, ALU.add) \
                .then_inc(s_own_keys, 1)
            dve.wait_ge(s_own_keys, 1)
            dve.tensor_scalar(neg_key[:, :], key_own[:, :], -1.0, None, ALU.mult).then_inc(s_own_keys, 1)

            dve.tensor_tensor(walks[:, :, :], walk_own[:, :].unsqueeze(1).broadcast_to([P, PASSES, GROUPS]),
                              pass_start[:, :].unsqueeze(2).broadcast_to([P, PASSES, GROUPS]), ALU.is_gt) \
                .then_inc(s_plan, 1)
            dve.wait_ge(s_plan, 1)
            dve.wait_ge(s_ones, 1)
            dve.tensor_reduce(walk_sum[:, :], walks[:, :, :], AX_X, ALU.add).then_inc(s_walk_sum, 1)
            dve.wait_ge(s_users_in, 1)
            dve.tensor_copy(users_in[:, :], p_q[0:1, 0:PASSES]).then_inc(s_plan, 1)
            dve.wait_ge(s_plan, 2)
            dve.tensor_tensor(pass_used[:, :, :], users_in[:, :].unsqueeze(1).broadcast_to([1, GROUPS, PASSES]),
                              group_start[:, :].unsqueeze(2).broadcast_to([1, GROUPS, PASSES]), ALU.is_gt) \
                .then_inc(s_plan, 1)
            dve.wait_ge(s_plan, 3)
            dve.tensor_reduce(n_pass[:, :], pass_used[:, :, :], AX_X, ALU.add).then_inc(s_plan, 1)
            dve.wait_ge(s_plan, 4)
            dve.tensor_scalar(n_pass[:, :], n_pass[:, :], 2.0, None, ALU.max).then_inc(s_plan, 1)
            dve.memset(first_pass[:, 0:1], 0).then_inc(s_plan, 1)
            dve.wait_ge(s_plan, 6)
            dve.tensor_tensor_scan(pass_end[:, :], n_pass[:, :], zeros16[:, :], 0.0, ALU.add, ALU.add) \
                .then_inc(s_plan, 1)
            dve.wait_ge(s_plan, 7)
            dve.tensor_copy(first_pass[:, 1:GROUPS + 1], pass_end[:, :]).then_inc(s_planned, 1)

            dve.wait_ge(s_key_row, 16)
            for j in range(HALF):
                if j:
                    dve.wait_ge(s_beats, j)
                dve.tensor_scalar(beats[:, :], key_row[:, :], key_own[:, j:j + 1], 0.0, ALU.is_gt, ALU.add,
                                  accum_out=rank_f[:, j:j + 1]).then_inc(s_beats, 1)

            dve.wait_ge(s_rows, 16)
            for n, (j0, j1, lo, hi) in enumerate(CLAMPS):
                x, y = row_sb[:, j0:j1, lo:hi], wrap[:, j0:j1, lo:hi]
                dve.tensor_scalar(y, x, 0.0, float(N), ALU.is_lt, ALU.mult).then_inc(s_wrap, 1)
                dve.wait_ge(s_wrap, 2 * n + 1)
                dve.scalar_tensor_tensor(x, x, float(N - 1), y, ALU.min, ALU.add).then_inc(s_wrap, 1)

            dve.wait_ge(s_signs, GROUPS - HALF)
            dve.tensor_scalar(rank_f[:, HALF:GROUPS], sign_sum[:, HALF:GROUPS], float(B - 1), 0.5,
                              ALU.add, ALU.mult).then_inc(s_beats, 1)
            dve.wait_ge(s_beats, HALF + 1)
            dve.tensor_copy(rank[:, :], rank_f[:, :]).then_inc(s_rank, 1)

            dve.wait_ge(s_weights, 16 * 23)
            dve.tensor_tensor(w_keys[E:P, 0:H0], w_keys[E:P, 0:H0], w_diff_hi[E:P, :], ALU.subtract).then_inc(s_wprep, 1)
            dve.tensor_tensor(w_q[0:E, 0:H0], w_q[0:E, 0:H0], w_diff_lo[:, :], ALU.add).then_inc(s_wprep, 1)
            dve.tensor_scalar(coslopes[:, :], slopes[:, :], -1.0, 1.0, ALU.mult, ALU.add).then_inc(s_wprep, 1)

            for n, ahead in enumerate((s_head_used, s_group, s_sum[1], *s_summed)):
                dve.memset(spare[:, n:n + 1], 0.0).then_inc(ahead, 1)

            def fill(k, i):
                rows_ = keys[k][:, 0:CHUNK, :]
                dve.wait_ge(s_got[k], (i + 1) * (16 * 2 * CHUNK))
                dve.tensor_tensor(rows_[:, :, E:P], got[k][:, 0, :, :], got[k][:, 1, :, :], ALU.add) \
                    .then_inc(s_summed[k], 1)
                dve.wait_ge(s_summed[k], i + 2)
                dve.tensor_tensor(rows_[:, :, 0:E], rows_[:, :, E:P],
                                  q_cur[:, :].unsqueeze(1).broadcast_to([P, CHUNK, E]), ALU.mult) \
                    .then_inc(s_keys[k], 1)

            def prelu(hid, neg, x, coslope, done):
                dve.scalar_tensor_tensor(hid, neg, coslope, x, ALU.mult, ALU.add).then_inc(done, 1)

            def prelu0(k, i):
                dve.wait_ge(s_neg0[k], i + 1)
                prelu(hid_0[k][:, :], neg_0[k][:, :], p_0[k][0:X0, :], coslopes[0:X0, 0:1], s_hid0[k])

            def prelu1(k, i):
                dve.wait_ge(s_neg1[k], i + 1)
                prelu(hid_1[k][:, :], neg_1[k][:, :], p_1[k][:, 0:PAIRS], coslopes[:, 1:2], s_hid1[k])

            def scores(k, i):
                o = 1 - k
                dve.tensor_scalar(open_[k][:, :], place[k][:, :], left[:, 0:1], HUGE, ALU.is_lt, ALU.mult) \
                    .then_inc(s_open[k], 1)
                dve.wait_ge(s_l2[k], i + 1)
                dve.wait_ge(s_open[k], i + 1)
                dve.scalar_tensor_tensor(score[k][:, 0:CHUNK], open_[k][:, :], MASKED,
                                         p_s[:, k * CHUNK:(k + 1) * CHUNK], ALU.add, ALU.min) \
                    .then_inc(s_masked[k], 1)
                if k == SLOTS - 1:
                    dve.tensor_scalar(left[:, :], left[:, :], -float(PASS), None, ALU.add).then_inc(s_left, 1)
                dve.wait_ge(s_masked[k], i + 1)
                dve.tensor_reduce(score[o][:, CHUNK:CHUNK + 1], score[k][:, :], AX_X, ALU.max) \
                    .then_inc(s_max[k], 1)
                dve.wait_ge(s_max[k], i + 1)
                dve.tensor_scalar(below[k][:, :], score[k][:, :], score[o][:, CHUNK:CHUNK + 1], None,
                                  ALU.subtract).then_inc(s_below[k], 1)

            def weigh(k, i):
                o = 1 - k
                dve.wait_ge(s_prob[k], i + 1)
                dve.wait_ge(s_sum[o], i + 1)
                if k == SLOTS - 1:
                    dve.wait_ge(s_left, i + 1)
                dve.tensor_tensor(part[k][:, :, :], keys[k][:, :, E:P + 1],
                                  prob[k][:, :].unsqueeze(2).broadcast_to([P, CHUNK + 1, W]), ALU.mult) \
                    .then_inc(s_part[k], 1)
                dve.wait_ge(s_part[k], i + 1)
                dve.tensor_reduce(keys[o][:, CHUNK, E:P + 1], part[k][:, :, :].rearrange("p t e -> p e t"),
                                  AX_X, ALU.add).then_inc(s_sum[k], 1)

            def step(k, i, before):
                fill(k, i)
                prelu1(*before)
                prelu0(k, i)
                scores(*before)
                weigh(*before)

            def finish(g, end):
                dve.wait_ge(s_sum[1], end + 1)
                dve.reciprocal(inv_sum[:, :], keys[0][:, CHUNK, P:P + 1]).then_inc(s_inv, 1)
                dve.wait_ge(s_inv, g + 1)
                dve.tensor_scalar(feat[:, bass.ds(g, 1), 3 * E:4 * E].rearrange("p a b -> p (a b)"),
                                  keys[0][:, CHUNK, E:P], inv_sum[:, 0:1], None, ALU.mult).then_inc(s_group, 1)

            def group(g, first, end, before):
                dve.wait_ge(s_head, (g + 1) * (16 * 3))
                dve.tensor_copy(q_cur[:, :], head[:, 1, :]).then_inc(s_q_cur, 1)
                dve.tensor_copy(feat[:, bass.ds(g, 1), 0:3 * E].rearrange("p a b -> p (a b)"),
                                head[:, :, :].rearrange("p a b -> p (a b)")).then_inc(s_taken, 1)
                dve.wait_ge(s_q_cur, g + 1)
                fill(0, first)
                if before:
                    prelu1(*before)
                prelu0(0, first)
                if before:
                    scores(*before)
                    weigh(*before)
                    finish(g - 1, first)
                dve.wait_ge(s_group, g + 1)
                dve.wait_ge(s_taken, g + 1)
                dve.memset(score[0][:, CHUNK:CHUNK + 1], -HUGE).then_inc(s_state, 1)
                dve.memset(keys[0][:, CHUNK, E:P + 1], 0.0).then_inc(s_state, 1)
                dve.wait_ge(s_head_idx, (g + 1) * 16)
                dve.tensor_copy(left[:, :], head_idx[:, 0:1]).then_inc(s_head_used, 1)
                dve.wait_ge(s_state, (g + 1) * 2)
                dve.wait_ge(s_head_used, g + 2)
                step(1, first, (0, first))
                with dve.Fori(first + 1, end) as i:
                    step(0, i, (1, i - 1))
                    step(1, i, (0, i))

            dve.wait_ge(s_planned, 1)
            group(0, 0, first_end(dve), None)
            with dve.Fori(1, GROUPS) as g:
                first, end = passes(dve, g)
                group(g, first, end, (1, first - 1))
            end = dve.value_load(first_pass[0:1, GROUPS:GROUPS + 1], min_val=2, max_val=GROUPS * PASSES)
            prelu1(1, end - 1)
            scores(1, end - 1)
            weigh(1, end - 1)
            finish(GROUPS - 1, end)

            for b in range(BATCHES):
                for x, xs, neg, hid, bias, cos, s_x, s_xs, s_neg, s_hid in (
                        (p_0, mx_0, mneg_0, mhid_0, mb_0, coslopes[0:M0, 2:3], s_m0, s_mx0, s_mneg0, s_mhid0),
                        (p_1, mx_1, mneg_1, mhid_1, mb_1, coslopes[0:M1, 3:4], s_m1, s_mx1, s_mneg1, s_mhid1)):
                    m = xs[0].shape[0]
                    dve.wait_ge(s_x, b + 1)
                    dve.tensor_scalar(xs[b % 2][:, :], x[b % 2][0:m, :], bias[:, 0:1], None, ALU.add) \
                        .then_inc(s_xs, 1)
                    dve.wait_ge(s_xs, b + 1)
                    dve.wait_ge(s_neg, b + 1)
                    prelu(hid[b % 2][0:m, :], neg[b % 2][:, :], xs[b % 2][:, :], cos, s_hid)


def kernel(**inputs):
    import numpy as np
    import concourse.bacc as bacc
    from concourse.bass_utils import run_bass_kernel_spmd as run

    x = {name: np.asarray(a) for name, a in inputs.items()}
    tags, artists = x["r_hist_tags"], x["r_hist_artists"]
    B, T = tags.shape
    hist = np.stack([tags.reshape(B, T // CHUNK, CHUNK), artists.reshape(B, T // CHUNK, CHUNK)], axis=2)
    own = np.stack([x["r_seq_lengths"], x["r_user_id"], x["r_target_tag"], x["r_target_artist"],
                    np.arange(B, dtype=np.int32)] + [np.zeros(B, np.int32)] * (META - 5), axis=1)
    arrays = {
        "lengths": x["r_seq_lengths"],
        "rows": np.concatenate([hist.reshape(B, 2 * T), own], axis=1),
        "user_table": x["L0_rec_user_table"], "tag_table": x["L0_rec_tag_table"],
        "artist_table": x["L0_rec_artist_table"],
    }
    for net in ("att", "mlp"):
        for n in range(3):
            arrays[f"{net}_w{n}"] = x[f"L0_rec_{net}_w{n}"].T
            arrays[f"{net}_b{n}"] = x[f"L0_rec_{net}_b{n}"]
            arrays[f"{net}_b{n}"] = arrays[f"{net}_b{n}"][:, None] if net == "mlp" and n < 2 \
                else arrays[f"{net}_b{n}"][None, :]
            if n < 2:
                arrays[f"{net}_a{n}"] = x[f"L0_rec_{net}_a{n}"]
    nc = bacc.Bacc("TRN2", target_bir_lowering=False, num_devices=1)
    arrays = {name: np.ascontiguousarray(a) for name, a in arrays.items()}
    t = {name: nc.dram_tensor(name, a.shape, mybir.dt.from_np(a.dtype), kind="ExternalInput").ap()
         for name, a in arrays.items()}
    keys_dram = nc.dram_tensor("keys_dram", (B,), F32, kind="Internal").ap()
    sorted_rows = nc.dram_tensor("sorted_rows", arrays["rows"].shape, I32, kind="Internal").ap()
    out = nc.dram_tensor("out", (B, 1), F32, kind="ExternalOutput").ap()
    net = [t[f"{n}_{p}"] for n in ("att", "mlp") for p in ("w0", "b0", "a0", "w1", "b1", "a1", "w2", "b2")]
    program(nc, t["lengths"], t["rows"], t["user_table"], t["tag_table"], t["artist_table"], *net,
            keys_dram, sorted_rows, out)
    return run(nc, [arrays], core_ids=[0]).results[0]["out"].reshape(B)
```

```python
from contextlib import ExitStack

import concourse.bass as bass
from concourse import mybir

F32 = mybir.dt.float32
I32 = mybir.dt.int32
U32 = mybir.dt.uint32
ALU = mybir.AluOpType
ACT = mybir.ActivationFunctionType
AX_X = mybir.AxisListType.X

P = 128
CHUNK = 4
SLOTS = 2
PASS = CHUNK * SLOTS
MASKED = -1000000000.0
HUGE = 3.0e38
META = 8
LENGTH, HOME = 3, 4


def program(nc, lengths, rows, user_table, tag_table, artist_table, a_w0, a_b0, a_a0, a_w1, a_b1, a_a1,
            a_w2, a_b2, m_w0, m_b0, m_a0, m_w1, m_b1, m_a1, m_w2, m_b2, keys_dram, sorted_rows, out):
    B, ROW = rows.shape
    T = (ROW - META) // 2
    N, E = tag_table.shape
    GROUPS = B // P
    H0, H1 = a_w0.shape[1], a_w1.shape[1]
    M0, M1 = m_w0.shape[1], m_w1.shape[1]
    PASSES = T // PASS
    COLS = CHUNK * P
    X0, X1 = H0 + 1, H1 + 1
    HALF_P = P // 2
    PAIRS = COLS // 2
    W = E + 1
    assert user_table.shape[0] == N and artist_table.shape[0] == N
    assert 2 * E == P and T % PASS == 0 and X0 <= P and X1 <= HALF_P and CHUNK == 4

    with ExitStack() as ctx:
        def sb(name, shape, dt=F32):
            return ctx.enter_context(nc.sbuf_tensor(name, shape, dt))

        def ps(name, shape):
            return ctx.enter_context(nc.psum_tensor(name, shape, F32))

        def sem(name):
            return ctx.enter_context(nc.semaphore(name))

        def sems(name):
            return [sem(f"{name}{k}") for k in range(SLOTS)]

        len_own = sb("len_own", [P, GROUPS], I32)
        tie_own = sb("tie_own", [P, GROUPS])
        full_own = sb("full_own", [P, GROUPS])
        walk_own = sb("walk_own", [P, GROUPS])
        key_own = sb("key_own", [P, GROUPS])
        neg_key = sb("neg_key", [P, GROUPS])
        key_row = sb("key_row", [P, B])
        beats = sb("beats", [P, B])
        signs = sb("signs", [P, B])
        sign_sum = sb("sign_sum", [P, GROUPS])
        rank_f = sb("rank_f", [P, GROUPS])
        rank = sb("rank", [P, GROUPS], U32)
        row_sb = sb("row_sb", [P, GROUPS, ROW], I32)
        wrap = sb("wrap", [P, GROUPS, ROW], I32)
        home = sb("home", [P, GROUPS, 2], I32)
        row_ids = sb("row_ids", [P, P])
        col_ids = sb("col_ids", [P, GROUPS])
        pass_start = sb("pass_start", [P, PASSES])
        walks = sb("walks", [P, PASSES, GROUPS])
        walk_sum = sb("walk_sum", [P, PASSES])
        ones = sb("ones", [P, P])
        group_start = sb("group_start", [P, GROUPS])
        users_in = sb("users_in", [P, PASSES])
        pass_used = sb("pass_used", [P, GROUPS, PASSES])
        n_pass = sb("n_pass", [P, GROUPS])
        zeros16 = sb("zeros16", [1, GROUPS])
        spare = sb("spare", [1, 16])
        pass_end = sb("pass_end", [1, GROUPS])
        first_pass = sb("first_pass", [1, GROUPS + 1], I32)
        before_last = sb("before_last", [P, GROUPS])
        top_len = sb("top_len", [1, GROUPS], I32)
        top_full = sb("top_full", [1, GROUPS])
        top_walk = sb("top_walk", [1, GROUPS])
        rest = sb("rest", [1, GROUPS])
        slot_rest = sb("slot_rest", [1, SLOTS, GROUPS])
        rest_number = sb("rest_number", [1, GROUPS], I32)
        rest_landed = sb("rest_landed", [1, SLOTS, GROUPS], I32)

        ident = sb("ident", [P, P])
        w_keys = sb("w_keys", [P, X0])
        w_diff_hi = sb("w_diff_hi", [P, H0])
        w_q = sb("w_q", [E + 1, X0])
        w_diff_lo = sb("w_diff_lo", [E, H0])
        w_1 = sb("w_1", [X0, HALF_P])
        w_2 = sb("w_2", [P, 2])
        slopes = sb("slopes", [P, 4])
        coslopes = sb("coslopes", [P, 4])
        mw_0 = sb("mw_0", [P, 2, M0])
        mb_0 = sb("mb_0", [M0, 1])
        mw_1 = sb("mw_1", [M0, M1])
        mb_1 = sb("mb_1", [M1, 1])
        mw_2 = sb("mw_2", [M1 + 1, 1])

        head_idx = sb("head_idx", [P, META], I32)
        head = sb("head", [P, 3, E])
        q_cur = sb("q_cur", [P, E])
        q_t = sb("q_t", [E + 1, P])
        left = sb("left", [P, 1])
        inv_sum = sb("inv_sum", [P, 1])
        feat = sb("feat", [P, 4 * E])

        stage = [sb(f"stage{k}", [P, 2 * CHUNK], I32) for k in range(SLOTS)]
        got = [sb(f"got{k}", [P, 2, CHUNK, E]) for k in range(SLOTS)]
        first_stage = [sb(f"first_stage{k}", [P, 2 * CHUNK], I32) for k in range(SLOTS)]
        first_got = [sb(f"first_got{k}", [P, 2, CHUNK, E]) for k in range(SLOTS)]
        keys = [sb(f"keys{k}", [P, CHUNK + 1, P + 1]) for k in range(SLOTS)]
        keys_t = [sb(f"keys_t{k}", [P, COLS]) for k in range(SLOTS)]
        neg_0 = [sb(f"neg_0{k}", [X0, COLS]) for k in range(SLOTS)]
        hid_0 = [sb(f"hid_0{k}", [X0, COLS]) for k in range(SLOTS)]
        neg_1 = [sb(f"neg_1{k}", [P, PAIRS]) for k in range(SLOTS)]
        hid_1 = [sb(f"hid_1{k}", [P, PAIRS]) for k in range(SLOTS)]
        place = [sb(f"place{k}", [P, CHUNK]) for k in range(SLOTS)]
        open_ = [sb(f"open{k}", [P, CHUNK]) for k in range(SLOTS)]
        score = [sb(f"score{k}", [P, CHUNK + 1]) for k in range(SLOTS)]
        below = [sb(f"below{k}", [P, CHUNK + 1]) for k in range(SLOTS)]
        prob = [sb(f"prob{k}", [P, CHUNK + 1]) for k in range(SLOTS)]
        part = [sb(f"part{k}", [P, CHUNK + 1, W]) for k in range(SLOTS)]

        feat_t = sb("feat_t", [P, 2, P])
        mx_0 = sb("mx_0", [M0, P])
        mneg_0 = sb("mneg_0", [M0, P])
        mhid_0 = sb("mhid_0", [M0, P])
        mx_1 = sb("mx_1", [M1, P])
        mneg_1 = sb("mneg_1", [M1, P])
        mhid_1 = sb("mhid_1", [M1 + 1, P])
        exp_z = sb("exp_z", [P, 1])
        result = sb("result", [P, 1])
        home_cur = sb("home_cur", [P, 2])
        in_row = sb("in_row", [P, P])
        in_col = sb("in_col", [P, GROUPS])
        results = sb("results", [P, GROUPS])

        p_t = [ps(f"p_t{k}", [P, COLS]) for k in range(SLOTS)]
        p_0 = [ps(f"p_0{k}", [P, COLS]) for k in range(SLOTS)]
        p_1 = [ps(f"p_1{k}", [P, COLS]) for k in range(SLOTS)]
        p_s = ps("p_s", [P, COLS])
        p_q = ps("p_q", [P, COLS])
        pm_t = p_q[:, P:3 * P]
        pm_0 = p_q[0:M0, 3 * P:4 * P]
        pm_1 = p_q[0:M1, P:2 * P]
        pm_2 = p_q[:, 2 * P:2 * P + 1]
        pm_home = p_q[:, 2 * P + 8:2 * P + 8 + GROUPS]

        s_len = sem("s_len")
        s_rows = sem("s_rows")
        s_const = sem("s_const")
        s_key = sem("s_key")
        s_own_keys = sem("s_own_keys")
        s_key_out = sem("s_key_out")
        s_key_row = sem("s_key_row")
        s_walk_sum = sem("s_walk_sum")
        s_users_in = sem("s_users_in")
        s_beats = sem("s_beats")
        s_signs = sem("s_signs")
        s_rank = sem("s_rank")
        s_wrap = sem("s_wrap")
        s_clamped = sem("s_clamped")
        s_scattered = sem("s_scattered")
        s_plan = sem("s_plan")
        s_planned = sem("s_planned")
        s_top_len = sem("s_top_len")
        s_top = sem("s_top")
        s_rest = sem("s_rest")
        s_home = sem("s_home")
        s_zeroed = sem("s_zeroed")
        s_weights = sem("s_weights")
        s_wprep = sem("s_wprep")
        s_ones = sem("s_ones")

        s_head_idx = sem("s_head_idx")
        s_target = sem("s_target")
        s_head = sem("s_head")
        s_left_set = sem("s_left_set")
        s_head_used = sem("s_head_used")
        s_q_cur = sem("s_q_cur")
        s_q_turned = sem("s_q_turned")
        s_q_t = sem("s_q_t")
        s_state = sem("s_state")
        s_left = sem("s_left")
        s_inv = sem("s_inv")
        s_group = sem("s_group")

        s_stage = sems("s_stage")
        s_got = sems("s_got")
        s_summed = sems("s_summed")
        s_first_stage = sems("s_first_stage")
        s_first_got = sems("s_first_got")
        s_first_summed = sems("s_first_summed")
        s_keys = sems("s_keys")
        s_turned = sems("s_turned")
        s_keys_t = sems("s_keys_t")
        s_l0 = sems("s_l0")
        s_neg0 = sems("s_neg0")
        s_hid0 = sems("s_hid0")
        s_l1 = sems("s_l1")
        s_neg1 = sems("s_neg1")
        s_hid1 = sems("s_hid1")
        s_l2 = sems("s_l2")
        s_open = sems("s_open")
        s_masked = sems("s_masked")
        s_max = sems("s_max")
        s_below = sems("s_below")
        s_prob = sems("s_prob")
        s_part = sems("s_part")
        s_sum = sems("s_sum")

        s_feat_t = sem("s_feat_t")
        s_feat_sb = sem("s_feat_sb")
        s_m0 = sem("s_m0")
        s_mx0 = sem("s_mx0")
        s_mneg0 = sem("s_mneg0")
        s_mhid0 = sem("s_mhid0")
        s_m1 = sem("s_m1")
        s_mx1 = sem("s_mx1")
        s_mneg1 = sem("s_mneg1")
        s_mhid1 = sem("s_mhid1")
        s_m2 = sem("s_m2")
        s_exp_z = sem("s_exp_z")
        s_home_cur = sem("s_home_cur")
        s_in_row = sem("s_in_row")
        s_in_col = sem("s_in_col")
        s_homed = sem("s_homed")
        s_placed = sem("s_placed")
        s_denom = sem("s_denom")
        s_result = sem("s_result")
        s_out = sem("s_out")

        AHEAD = 8
        LANDED = 16 * 2 * CHUNK
        OURS = GROUPS * 7 // 16

        NUMBERS = 2 * T + 3

        block = ctx.enter_context(nc.Block())

        def passes(eng, g):
            a = eng.value_load(first_pass[0:1, bass.ds(g, 1)], min_val=0, max_val=GROUPS * PASSES)
            b = eng.value_load(first_pass[0:1, bass.ds(g + 1, 1)], min_val=0, max_val=GROUPS * PASSES)
            return a, b

        def first_landed(eng, g, k):
            return eng.value_load(rest_landed[0:1, k, bass.ds(g, 1)], min_val=0, max_val=LANDED)

        def first_end(eng):
            return eng.value_load(first_pass[0:1, 1:2], min_val=2, max_val=PASSES)

        @block.sync
        def _(sp):
            sp.dma_start(len_own[:, :], lengths.rearrange("(p j) -> p j", p=P)).then_inc(s_len, 16)
            sp.wait_ge(s_own_keys, 1)
            sp.dma_start(keys_dram.rearrange("(p j) -> p j", p=P), key_own[:, :]).then_inc(s_key_out, 16)
            sp.wait_ge(s_key_out, 16)
            sp.dma_start(key_row[:, :], keys_dram.partition_broadcast(P)).then_inc(s_key_row, 16)
            sp.dma_start(row_sb[:, :, :], rows.rearrange("(p j) c -> p j c", p=P)).then_inc(s_rows, 16)

            sp.wait_ge(s_zeroed, 1)
            sp.wait_ge(s_ones, 1)
            loads = [
                (w_keys[0:E, 0:H0], a_w0[3 * E:4 * E, :]), (w_keys[E:P, 0:H0], a_w0[E:2 * E, :]),
                (w_diff_hi[E:P, :], a_w0[2 * E:3 * E, :]), (w_diff_lo[:, :], a_w0[2 * E:3 * E, :]),
                (w_q[0:E, 0:H0], a_w0[0:E, :]), (w_q[E:E + 1, 0:H0], a_b0),
                (w_1[0:H0, 0:H1], a_w1), (w_1[H0:X0, 0:H1], a_b1), (w_1[H0:X0, H1:X1], ones[0:1, 0:1]),
                (w_2[0:H1, 0:1], a_w2), (w_2[H1:X1, 0:1], a_b2),
                (w_2[HALF_P:HALF_P + H1, 1:2], a_w2), (w_2[HALF_P + H1:HALF_P + X1, 1:2], a_b2),
                (mw_0[:, :, :], m_w0.rearrange("(h k) n -> k h n", h=2)), (mw_1[:, :], m_w1),
                (mw_2[0:M1, :], m_w2), (mw_2[M1:M1 + 1, :], m_b2),
                (mb_0[:, :], m_b0), (mb_1[:, :], m_b1),
            ]
            for dst, src in loads:
                sp.dma_start(dst, src).then_inc(s_weights, 16)
            for n, a in enumerate((a_a0, a_a1, m_a0, m_a1)):
                sp.dma_start(slopes[:, n:n + 1], a.partition_broadcast(P)).then_inc(s_weights, 16)

            sp.wait_ge(s_scattered, 16 * GROUPS)
            sp.wait_ge(s_planned, 1)

            heads, landed = (sp.alloc_register(name) for name in ("heads", "landed"))
            landed_first = [sp.alloc_register(f"landed_first{k}") for k in range(SLOTS)]
            for register in (heads, *landed_first):
                sp.reg_mov(register, 0)
            sp.reg_mov(landed, 16)

            def load_stage(tile, done, g, number, k):
                col = nc.s_assert_within(number * (2 * PASS), 0, (PASSES - 1) * (2 * PASS),
                                         skip_runtime_bounds_check_because="a group has at most PASSES passes")
                sp.dma_start(tile[:, :], sorted_rows[bass.ds(g * P, P), bass.ds(col + 2 * CHUNK * k, 2 * CHUNK)]) \
                    .then_inc(done, 16)

            def group(g, first, end):
                again = not isinstance(first, int)
                sp.reg_add(heads, heads, 1)
                sp.wait_ge(s_planned, 1)
                sp.wait_ge(s_head_used, heads)
                sp.dma_start(head_idx[:, :], sorted_rows[bass.ds(g * P, P), 2 * T:2 * T + META]) \
                    .then_inc(s_head_idx, 16)
                for k in range(SLOTS):
                    if again:
                        sp.wait_ge(s_planned, 1)
                        sp.wait_ge(s_first_stage[k], g * 16)
                        sp.wait_ge(s_first_got[k], landed_first[k])
                    load_stage(first_stage[k], s_first_stage[k], g, end - 1 - first, k)
                    sp.reg_add(landed_first[k], landed_first[k], first_landed(sp, g, k) if again else LANDED)
                if not again:
                    places = sorted_rows.rearrange("(g p) c -> p g c", p=P)
                    with nc.allow_non_contiguous_dma(reason="one word per user, once"):
                        sp.dma_start(top_len[:, :], places[0:1, :, 2 * T + LENGTH]).then_inc(s_top_len, 16)
                        sp.dma_start(home[:, :, :], places[:, :, 2 * T + HOME:2 * T + HOME + 2]).then_inc(s_home, 16)
                with sp.Fori(first + 1, end) as i:
                    for k in range(SLOTS):
                        sp.wait_ge(s_planned, 1)
                        sp.wait_ge(s_got[k], landed)
                        load_stage(stage[k], s_stage[k], g, end - 1 - i, k)
                    sp.reg_add(landed, landed, LANDED)

            group(0, 0, first_end(sp))
            sp.wait_ge(s_rest, 2)
            with sp.Fori(1, GROUPS) as g:
                group(g, *passes(sp, g))

            sp.wait_ge(s_placed, GROUPS)
            sp.dma_start(out.rearrange("(p j) c -> p (j c)", p=P), results[:, :]).then_inc(s_out, 16)
            sp.wait_ge(s_out, 16)

        @block.gpsimd
        def _(pool):
            pool.iota(tie_own[:, :], [[-1, GROUPS]], base=B - 1, channel_multiplier=-GROUPS,
                      allow_small_or_imprecise_dtypes=True).then_inc(s_const, 1)
            pool.iota(pass_start[:, :], [[PASS, PASSES]], base=0, channel_multiplier=0,
                      allow_small_or_imprecise_dtypes=True).then_inc(s_const, 1)
            pool.iota(group_start[:, :], [[P, GROUPS]], base=0, channel_multiplier=0,
                      allow_small_or_imprecise_dtypes=True).then_inc(s_const, 1)
            for k in range(SLOTS):
                pool.iota(place[k][:, :], [[1, CHUNK]], base=CHUNK * k, channel_multiplier=0,
                          allow_small_or_imprecise_dtypes=True).then_inc(s_const, 1)
            pool.iota(row_ids[:, :], [[1, P]], base=0, channel_multiplier=0,
                      allow_small_or_imprecise_dtypes=True).then_inc(s_const, 1)
            pool.iota(col_ids[:, :], [[1, GROUPS]], base=0, channel_multiplier=0,
                      allow_small_or_imprecise_dtypes=True).then_inc(s_const, 1)
            pool.memset(ident[:, :], 0.0).then_inc(s_const, 1)
            pool.wait_ge(s_const, 8)
            pool.affine_select(out=ident[:, :], in_=ident[:, :], compare_op=ALU.not_equal, fill=1.0,
                               base=0, pattern=[[-1, P]], channel_multiplier=1).then_inc(s_const, 1)
            for n, ahead in enumerate(s_got):
                pool.dma_start(spare[0:1, AHEAD + n:AHEAD + n + 1], group_start[0:1, 0:1]).then_inc(ahead, 16)
            pool.wait_ge(s_rank, 1)
            for j in range(GROUPS):
                pool.wait_ge(s_clamped, j + 1)
                pool.indirect_dma_start(
                    out=sorted_rows, out_offset=bass.IndirectOffsetOnAxis(ap=rank[:, j:j + 1], axis=0),
                    in_=row_sb[:, j, :], in_offset=None).then_inc(s_scattered, 16)

            head_loads, turn, loads = (pool.alloc_register(name) for name in ("head_loads", "turn", "loads"))
            groups = pool.alloc_register("groups")
            for register in (head_loads, turn, loads, groups):
                pool.reg_mov(register, 0)
            pool.wait_ge(s_planned, 1)

            def gather(tile, by, k, t, done):
                for n, table in enumerate((tag_table, artist_table)):
                    c = n * CHUNK + t
                    pool.indirect_dma_start(
                        out=tile[k][:, n, t, :], out_offset=None, in_=table,
                        in_offset=bass.IndirectOffsetOnAxis(ap=by[k][:, c:c + 1].bitcast(U32), axis=0)) \
                        .then_inc(done[k], 16)

            def gather_first(positions):
                for k in range(SLOTS):
                    pool.wait_ge(s_planned, 1)
                    pool.wait_ge(s_first_stage[k], head_loads)
                    pool.wait_ge(s_first_summed[k], groups)
                    for t in range(CHUNK):
                        if positions is None:
                            gather(first_got, first_stage, k, t, s_first_got)
                        else:
                            with pool.If(positions > k * CHUNK + t):
                                gather(first_got, first_stage, k, t, s_first_got)

            def gather_pass():
                pool.reg_add(turn, turn, 1)
                pool.reg_add(loads, loads, 16)
                for k in range(SLOTS):
                    pool.wait_ge(s_planned, 1)
                    pool.wait_ge(s_stage[k], loads)
                    pool.wait_ge(s_summed[k], turn)
                    for t in range(CHUNK):
                        gather(got, stage, k, t, s_got)

            def gather_head(n, table, done):
                pool.indirect_dma_start(
                    out=head[:, n, :], out_offset=None, in_=table,
                    in_offset=bass.IndirectOffsetOnAxis(ap=head_idx[:, n:n + 1].bitcast(U32), axis=0)) \
                    .then_inc(done, 16)

            def group(g, whole):
                first, end = passes(pool, g)
                pool.reg_add(head_loads, head_loads, 16)
                pool.reg_add(groups, groups, 1)
                pool.wait_ge(s_planned, 1)
                pool.wait_ge(s_head_idx, head_loads)
                gather_head(1, tag_table, s_target)
                gather_first(None if whole
                             else pool.value_load(rest_number[0:1, bass.ds(g, 1)], min_val=-T, max_val=PASS))
                gather_head(0, user_table, s_head)
                gather_head(2, artist_table, s_head)
                with pool.Fori(first + 1, end):
                    gather_pass()

            group(0, True)
            pool.wait_ge(s_rest, 1)
            with pool.Fori(1, GROUPS) as g:
                group(g, False)

        @block.scalar
        def _(act):
            act.wait_ge(s_key_row, 16)
            act.wait_ge(s_own_keys, 2)
            for j in range(OURS, GROUPS):
                if j > OURS:
                    act.wait_ge(s_signs, j - OURS)
                act.activation(signs[:, :], key_row[:, :], ACT.Sign, bias=neg_key[:, j:j + 1],
                               accum_out=sign_sum[:, j:j + 1]).then_inc(s_signs, 1)
            for j in range(GROUPS):
                x = row_sb[:, j, 0:NUMBERS]
                act.wait_ge(s_wrap, 2 * j + 2)
                act.activation(x, x, ACT.Relu).then_inc(s_clamped, 1)

            def turn(k, i):
                act.wait_ge(s_turned[k], i + 1)
                act.activation(keys_t[k][:, :], p_t[k][:, :], ACT.Copy).then_inc(s_keys_t[k], 1)

            def relu0(k, i):
                act.wait_ge(s_l0[k], i + 1)
                act.activation(neg_0[k][:, :], p_0[k][0:X0, :], ACT.Relu, scale=-1.0).then_inc(s_neg0[k], 1)

            def relu1(k, i):
                act.wait_ge(s_l1[k], i + 1)
                act.activation(neg_1[k][:, :], p_1[k][:, 0:PAIRS], ACT.Relu, scale=-1.0).then_inc(s_neg1[k], 1)

            def exp(k, i):
                act.wait_ge(s_below[k], i + 1)
                act.activation(prob[k][:, :], below[k][:, :], ACT.Exp).then_inc(s_prob[k], 1)

            def step(k, i, before):
                relu1(*before)
                turn(k, i)
                exp(*before)
                relu0(k, i)

            def mlp_features(m):
                act.wait_ge(s_feat_t, m + 1)
                act.activation(feat_t[:, :, :].rearrange("p h b -> p (h b)"), pm_t, ACT.Copy).then_inc(s_feat_sb, 1)

            def mlp_relu0(m):
                act.wait_ge(s_mx0, m + 1)
                act.activation(mneg_0[:, :], mx_0[:, :], ACT.Relu, scale=-1.0).then_inc(s_mneg0, 1)

            def mlp_relu1(m):
                act.wait_ge(s_mx1, m + 1)
                act.activation(mneg_1[:, :], mx_1[:, :], ACT.Relu, scale=-1.0).then_inc(s_mneg1, 1)

            def mlp_exp(m):
                act.wait_ge(s_m2, m + 1)
                act.activation(exp_z[:, :], pm_2, ACT.Exp, scale=-1.0).then_inc(s_exp_z, 1)

            def group(g, first, end, before, older):
                if older:
                    mlp_relu1(g - 2)
                if before:
                    relu1(*before)
                act.wait_ge(s_q_turned, g + 1)
                act.activation(q_t[0:E, :], p_q[0:E, 0:P], ACT.Copy).then_inc(s_q_t, 1)
                turn(0, first)
                if older:
                    mlp_exp(g - 2)
                if before:
                    exp(*before)
                relu0(0, first)
                relu1(0, first)
                turn(1, first)
                if before:
                    mlp_features(g - 1)
                exp(0, first)
                if before:
                    mlp_relu0(g - 1)
                relu0(1, first)
                with act.Fori(first + 1, end) as i:
                    step(0, i, (1, i - 1))
                    step(1, i, (0, i))

            act.wait_ge(s_planned, 1)
            group(0, 0, first_end(act), None, False)
            first, end = passes(act, 1)
            group(1, first, end, (1, first - 1), False)
            with act.Fori(2, GROUPS) as g:
                first, end = passes(act, g)
                group(g, first, end, (1, first - 1), True)
            end = act.value_load(first_pass[0:1, GROUPS:GROUPS + 1], min_val=2, max_val=GROUPS * PASSES)
            mlp_relu1(GROUPS - 2)
            relu1(1, end - 1)
            mlp_exp(GROUPS - 2)
            exp(1, end - 1)
            mlp_features(GROUPS - 1)
            mlp_relu0(GROUPS - 1)
            mlp_relu1(GROUPS - 1)
            mlp_exp(GROUPS - 1)

        @block.tensor
        def _(pe):
            pe.wait_ge(s_walk_sum, 1)
            pe.matmul(p_q[:, 0:PASSES], ones[:, :], walk_sum[:, :], start=True, stop=True).then_inc(s_users_in, 1)
            pe.wait_ge(s_const, 9)
            pe.wait_ge(s_wprep, 2)
            pe.wait_ge(s_ones, 1)

            def turn(k, i):
                pe.wait_ge(s_keys[k], i + 1)
                for t in range(CHUNK):
                    mm = pe.transpose(p_t[k][:, t * P:(t + 1) * P], keys[k][:, t, 0:P], ident[:, :])
                mm.then_inc(s_turned[k], 1)

            def target(k):
                pe.matmul(p_0[k][0:X0, :], w_q[:, :], q_t[:, :].unsqueeze(1).broadcast_to([E + 1, CHUNK, P]),
                          start=True, stop=False)

            def layer0(k, i):
                pe.wait_ge(s_keys_t[k], i + 1)
                pe.matmul(p_0[k][0:X0, :], w_keys[:, :], keys_t[k][:, :],
                          start=False, stop=True).then_inc(s_l0[k], 1)

            def layer1(k, i):
                by_parity = hid_0[k][:, :].rearrange("h (t s b) -> h s t b", s=2, b=P)
                pe.wait_ge(s_hid0[k], i + 1)
                for s in range(2):
                    mm = pe.matmul(p_1[k][s * HALF_P:(s + 1) * HALF_P, 0:PAIRS], w_1[:, :], by_parity[:, s],
                                   start=True, stop=True)
                mm.then_inc(s_l1[k], 1)

            def layer2(k, i):
                pe.wait_ge(s_hid1[k], i + 1)
                for t in range(0, CHUNK, 2):
                    c = k * CHUNK + t
                    mm = pe.matmul(p_s[:, c:c + 2], hid_1[k][:, t * P // 2:(t + 2) * P // 2], w_2[:, :],
                                   start=True, stop=True)
                mm.then_inc(s_l2[k], 1)

            def step(k, i, before):
                turn(k, i)
                if k == 0:
                    target(0)
                layer2(*before)
                layer0(k, i)
                if k == 0:
                    target(1)
                layer1(k, i)

            def mlp_features(m):
                pe.wait_ge(s_planned, 1)
                pe.wait_ge(s_group, m + 2)
                for h in range(2):
                    mm = pe.transpose(pm_t[:, h * P:(h + 1) * P], feat[:, h * P:(h + 1) * P], ident[:, :])
                mm.then_inc(s_feat_t, 1)

            def mlp_layer0(m):
                pe.wait_ge(s_feat_sb, m + 1)
                for h in range(2):
                    mm = pe.matmul(pm_0, mw_0[:, h, :], feat_t[:, h, :], start=h == 0, stop=h == 1)
                mm.then_inc(s_m0, 1)

            def mlp_layer1(m):
                pe.wait_ge(s_mhid0, m + 1)
                pe.matmul(pm_1, mw_1[:, :], mhid_0[:, :], start=True, stop=True).then_inc(s_m1, 1)

            def mlp_layer2(m):
                pe.wait_ge(s_mhid1, m + 1)
                pe.matmul(pm_2, mhid_1[:, :], mw_2[:, :], start=True, stop=True).then_inc(s_m2, 1)

            def spread(m):
                pe.wait_ge(s_in_col, m + 1)
                pe.matmul(pm_home, in_row[:, :], in_col[:, :], start=True, stop=True).then_inc(s_homed, 1)

            def group(g, first, end, before, older):
                pe.wait_ge(s_planned, 1)
                pe.wait_ge(s_q_cur, g + 1)
                pe.transpose(p_q[0:E, 0:P], q_cur[:, :], ident[:, :]).then_inc(s_q_turned, 1)
                turn(0, first)
                pe.wait_ge(s_q_t, g + 1)
                target(0)
                if older:
                    mlp_layer2(g - 2)
                if before:
                    layer2(*before)
                layer0(0, first)
                target(1)
                if older:
                    spread(g - 2)
                layer1(0, first)
                turn(1, first)
                if older:
                    pe.wait_ge(s_placed, g - 1)
                if before:
                    mlp_features(g - 1)
                layer2(0, first)
                if before:
                    mlp_layer0(g - 1)
                layer0(1, first)
                if before:
                    mlp_layer1(g - 1)
                layer1(1, first)
                with pe.Fori(first + 1, end) as i:
                    step(0, i, (1, i - 1))
                    step(1, i, (0, i))

            pe.wait_ge(s_planned, 1)
            group(0, 0, first_end(pe), None, False)
            first, end = passes(pe, 1)
            group(1, first, end, (1, first - 1), False)
            with pe.Fori(2, GROUPS) as g:
                first, end = passes(pe, g)
                group(g, first, end, (1, first - 1), True)
            end = pe.value_load(first_pass[0:1, GROUPS:GROUPS + 1], min_val=2, max_val=GROUPS * PASSES)
            mlp_layer2(GROUPS - 2)
            layer2(1, end - 1)
            spread(GROUPS - 2)
            pe.wait_ge(s_placed, GROUPS - 1)

            mlp_features(GROUPS - 1)
            mlp_layer0(GROUPS - 1)
            mlp_layer1(GROUPS - 1)
            mlp_layer2(GROUPS - 1)
            spread(GROUPS - 1)

        @block.vector
        def _(dve):
            for tile in (w_keys, w_q, w_1, w_2):
                ins = dve.memset(tile[:, :], 0.0)
            ins.then_inc(s_zeroed, 1)
            dve.wait_ge(s_zeroed, 1)
            dve.memset(w_q[E:E + 1, H0:X0], 1.0)
            for tile, row in ((q_t, E), (mhid_1, M1)):
                dve.memset(tile[row:row + 1, :], 1.0)
            for k in range(SLOTS):
                dve.memset(keys[k][:, :, P:P + 1], 1.0)
            dve.memset(ones[:, :], 1.0)
            dve.memset(results[:, :], 0.0)
            dve.memset(zeros16[:, :], 0.0).then_inc(s_ones, 1)

            dve.wait_ge(s_len, 16)
            dve.wait_ge(s_const, 7)
            dve.tensor_scalar(full_own[:, :], len_own[:, :], 0.0, float(T), ALU.is_le, ALU.mult).then_inc(s_key, 1)
            dve.tensor_scalar(walk_own[:, :], len_own[:, :], 0.0, float(T), ALU.max, ALU.min).then_inc(s_key, 1)
            dve.wait_ge(s_key, 2)
            dve.tensor_tensor(walk_own[:, :], full_own[:, :], walk_own[:, :], ALU.add).then_inc(s_key, 1)
            dve.wait_ge(s_key, 3)
            dve.scalar_tensor_tensor(key_own[:, :], walk_own[:, :], float(B), tie_own[:, :], ALU.mult, ALU.add) \
                .then_inc(s_own_keys, 1)
            dve.wait_ge(s_own_keys, 1)
            dve.tensor_scalar(neg_key[:, :], key_own[:, :], -1.0, None, ALU.mult).then_inc(s_own_keys, 1)

            dve.tensor_tensor(walks[:, :, :], walk_own[:, :].unsqueeze(1).broadcast_to([P, PASSES, GROUPS]),
                              pass_start[:, :].unsqueeze(2).broadcast_to([P, PASSES, GROUPS]), ALU.is_gt) \
                .then_inc(s_plan, 1)
            dve.wait_ge(s_plan, 1)
            dve.wait_ge(s_ones, 1)
            dve.tensor_reduce(walk_sum[:, :], walks[:, :, :], AX_X, ALU.add).then_inc(s_walk_sum, 1)
            dve.wait_ge(s_users_in, 1)
            dve.tensor_copy(users_in[:, :], p_q[:, 0:PASSES]).then_inc(s_plan, 1)
            dve.wait_ge(s_plan, 2)
            dve.tensor_tensor(pass_used[:, :, :], users_in[:, :].unsqueeze(1).broadcast_to([P, GROUPS, PASSES]),
                              group_start[:, :].unsqueeze(2).broadcast_to([P, GROUPS, PASSES]), ALU.is_gt) \
                .then_inc(s_plan, 1)
            dve.wait_ge(s_plan, 3)
            dve.tensor_reduce(n_pass[:, :], pass_used[:, :, :], AX_X, ALU.add).then_inc(s_plan, 1)
            dve.wait_ge(s_plan, 4)
            dve.tensor_scalar(n_pass[:, :], n_pass[:, :], 2.0, None, ALU.max).then_inc(s_plan, 1)
            dve.memset(first_pass[:, 0:1], 0).then_inc(s_plan, 1)
            dve.wait_ge(s_plan, 6)
            dve.tensor_scalar(before_last[:, :], n_pass[:, :], -1.0, float(PASS), ALU.add, ALU.mult).then_inc(s_plan, 1)
            dve.tensor_tensor_scan(pass_end[:, :], n_pass[0:1, :], zeros16[:, :], 0.0, ALU.add, ALU.add) \
                .then_inc(s_plan, 1)
            dve.wait_ge(s_plan, 8)
            dve.tensor_copy(first_pass[:, 1:GROUPS + 1], pass_end[:, :]).then_inc(s_planned, 1)

            dve.wait_ge(s_key_row, 16)
            for j in range(OURS):
                if j:
                    dve.wait_ge(s_beats, j)
                dve.tensor_scalar(beats[:, :], key_row[:, :], key_own[:, j:j + 1], 0.0, ALU.is_gt, ALU.add,
                                  accum_out=rank_f[:, j:j + 1]).then_inc(s_beats, 1)

            dve.wait_ge(s_rows, 16)
            for j in range(GROUPS):
                x, y = row_sb[:, j, 0:NUMBERS], wrap[:, j, 0:NUMBERS]
                dve.tensor_scalar(y, x, 0.0, float(N), ALU.is_lt, ALU.mult).then_inc(s_wrap, 1)
                dve.wait_ge(s_wrap, 2 * j + 1)
                dve.scalar_tensor_tensor(x, x, float(N - 1), y, ALU.min, ALU.add).then_inc(s_wrap, 1)
                if j == 0:
                    dve.wait_ge(s_signs, GROUPS - OURS)
                    dve.tensor_scalar(rank_f[:, OURS:GROUPS], sign_sum[:, OURS:GROUPS], float(B - 1), 0.5,
                                      ALU.add, ALU.mult).then_inc(s_beats, 1)
                    dve.wait_ge(s_beats, OURS + 1)
                    dve.tensor_copy(rank[:, :], rank_f[:, :]).then_inc(s_rank, 1)

            dve.wait_ge(s_weights, 16 * 23)
            dve.tensor_tensor(w_keys[E:P, 0:H0], w_keys[E:P, 0:H0], w_diff_hi[E:P, :], ALU.subtract) \
                .then_inc(s_wprep, 1)
            dve.tensor_tensor(w_q[0:E, 0:H0], w_q[0:E, 0:H0], w_diff_lo[:, :], ALU.add).then_inc(s_wprep, 1)
            dve.tensor_scalar(coslopes[:, :], slopes[:, :], -1.0, 1.0, ALU.mult, ALU.add).then_inc(s_wprep, 1)

            for n, ahead in enumerate((s_head_used, s_group, s_sum[1], *s_summed, *s_first_summed)):
                dve.memset(spare[:, n:n + 1], 0.0).then_inc(ahead, 1)

            landed_first = [dve.alloc_register(f"landed_first{k}") for k in range(SLOTS)]
            landed, summed = (dve.alloc_register(name) for name in ("landed", "summed"))
            for register in landed_first:
                dve.reg_mov(register, 0)
            dve.reg_mov(landed, 16)
            dve.reg_mov(summed, 1)

            def fill(k, tile, done, count):
                rows_ = keys[k][:, 0:CHUNK, :]
                dve.tensor_tensor(rows_[:, :, E:P], tile[:, 0, :, :], tile[:, 1, :, :], ALU.add).then_inc(done, 1)
                dve.wait_ge(s_planned, 1)
                dve.wait_ge(done, count)
                dve.tensor_tensor(rows_[:, :, 0:E], rows_[:, :, E:P],
                                  q_cur[:, :].unsqueeze(1).broadcast_to([P, CHUNK, E]), ALU.mult) \
                    .then_inc(s_keys[k], 1)

            def fill_first(k, g, adds):
                dve.reg_add(landed_first[k], landed_first[k], adds)
                dve.wait_ge(s_planned, 1)
                dve.wait_ge(s_first_got[k], landed_first[k])
                fill(k, first_got[k], s_first_summed[k], g + 2)

            def prelu(hid, neg, x, coslope, done):
                dve.scalar_tensor_tensor(hid, neg, coslope, x, ALU.mult, ALU.add).then_inc(done, 1)

            def prelu0(k, i):
                dve.wait_ge(s_neg0[k], i + 1)
                prelu(hid_0[k][:, :], neg_0[k][:, :], p_0[k][0:X0, :], coslopes[0:X0, 0:1], s_hid0[k])

            def prelu1(k, i):
                dve.wait_ge(s_neg1[k], i + 1)
                prelu(hid_1[k][:, :], neg_1[k][:, :], p_1[k][:, 0:PAIRS], coslopes[:, 1:2], s_hid1[k])

            def scores(k, i):
                o = 1 - k
                dve.tensor_scalar(open_[k][:, :], place[k][:, :], left[:, 0:1], HUGE, ALU.is_lt, ALU.mult) \
                    .then_inc(s_open[k], 1)
                dve.wait_ge(s_l2[k], i + 1)
                dve.wait_ge(s_open[k], i + 1)
                dve.scalar_tensor_tensor(score[k][:, 0:CHUNK], open_[k][:, :], MASKED,
                                         p_s[:, k * CHUNK:(k + 1) * CHUNK], ALU.add, ALU.min) \
                    .then_inc(s_masked[k], 1)
                if k == SLOTS - 1:
                    dve.tensor_scalar(left[:, :], left[:, :], float(PASS), None, ALU.add).then_inc(s_left, 1)
                dve.wait_ge(s_masked[k], i + 1)
                dve.tensor_reduce(score[o][:, CHUNK:CHUNK + 1], score[k][:, :], AX_X, ALU.max) \
                    .then_inc(s_max[k], 1)
                dve.wait_ge(s_max[k], i + 1)
                dve.tensor_scalar(below[k][:, :], score[k][:, :], score[o][:, CHUNK:CHUNK + 1], None,
                                  ALU.subtract).then_inc(s_below[k], 1)

            def weigh(k, i):
                o = 1 - k
                dve.wait_ge(s_prob[k], i + 1)
                dve.wait_ge(s_sum[o], i + 1)
                if k == SLOTS - 1:
                    dve.wait_ge(s_left, i + 1)
                dve.tensor_tensor(part[k][:, :, :], keys[k][:, :, E:P + 1],
                                  prob[k][:, :].unsqueeze(2).broadcast_to([P, CHUNK + 1, W]), ALU.mult) \
                    .then_inc(s_part[k], 1)
                dve.wait_ge(s_part[k], i + 1)
                dve.tensor_reduce(keys[o][:, CHUNK, E:P + 1], part[k][:, :, :].rearrange("p t e -> p e t"),
                                  AX_X, ALU.add).then_inc(s_sum[k], 1)

            def step(k, i, before):
                if k == 0:
                    dve.reg_add(landed, landed, LANDED)
                    dve.reg_add(summed, summed, 1)
                dve.wait_ge(s_planned, 1)
                dve.wait_ge(s_got[k], landed)
                fill(k, got[k], s_summed[k], summed)
                prelu1(*before)
                scores(*before)
                weigh(*before)
                prelu0(k, i)

            def mlp_prelu0(m):
                dve.wait_ge(s_m0, m + 1)
                dve.tensor_scalar(mx_0[:, :], pm_0, mb_0[:, 0:1], None, ALU.add).then_inc(s_mx0, 1)
                dve.wait_ge(s_mx0, m + 1)
                dve.wait_ge(s_mneg0, m + 1)
                prelu(mhid_0[:, :], mneg_0[:, :], mx_0[:, :], coslopes[0:M0, 2:3], s_mhid0)

            def mlp_prelu1(m):
                dve.wait_ge(s_m1, m + 1)
                dve.tensor_scalar(mx_1[:, :], pm_1, mb_1[:, 0:1], None, ALU.add).then_inc(s_mx1, 1)
                dve.wait_ge(s_mx1, m + 1)
                dve.wait_ge(s_mneg1, m + 1)
                prelu(mhid_1[0:M1, :], mneg_1[:, :], mx_1[:, :], coslopes[0:M1, 3:4], s_mhid1)

            def mlp_home(m):
                dve.wait_ge(s_home, 16)
                dve.tensor_copy(home_cur[:, :], home[:, bass.ds(m, 1), :].rearrange("p a b -> p (a b)")) \
                    .then_inc(s_home_cur, 1)
                dve.wait_ge(s_home_cur, m + 1)
                dve.tensor_scalar(in_row[:, :], row_ids[:, :], home_cur[:, 0:1], None, ALU.is_equal) \
                    .then_inc(s_in_row, 1)

            def mlp_result(m):
                dve.wait_ge(s_exp_z, m + 1)
                dve.tensor_scalar(exp_z[:, :], exp_z[:, :], 1.0, None, ALU.add).then_inc(s_denom, 1)
                dve.wait_ge(s_denom, m + 1)
                dve.reciprocal(result[:, :], exp_z[:, :]).then_inc(s_result, 1)
                dve.wait_ge(s_result, m + 1)
                dve.wait_ge(s_in_row, m + 1)
                dve.tensor_scalar(in_col[:, :], col_ids[:, :], home_cur[:, 1:2], result[:, 0:1],
                                  ALU.is_equal, ALU.mult).then_inc(s_in_col, 1)

            def mlp_place(m):
                dve.wait_ge(s_homed, m + 1)
                dve.tensor_tensor(results[:, :], results[:, :], pm_home, ALU.add).then_inc(s_placed, 1)

            def finish(g, end):
                dve.wait_ge(s_sum[1], end + 1)
                dve.reciprocal(inv_sum[:, :], keys[0][:, CHUNK, P:P + 1]).then_inc(s_inv, 1)
                dve.wait_ge(s_inv, g + 1)
                dve.wait_ge(s_head_used, g + 2)
                dve.tensor_scalar(feat[:, 3 * E:4 * E],
                                  keys[0][:, CHUNK, E:P], inv_sum[:, 0:1], None, ALU.mult).then_inc(s_group, 1)

            def count_rest():
                dve.wait_ge(s_top_len, 16)
                dve.tensor_scalar(top_full[:, :], top_len[:, :], 0.0, float(T), ALU.is_le, ALU.mult).then_inc(s_top, 1)
                dve.tensor_scalar(top_walk[:, :], top_len[:, :], 0.0, float(T), ALU.max, ALU.min).then_inc(s_top, 1)
                dve.wait_ge(s_top, 2)
                dve.tensor_tensor(top_walk[:, :], top_walk[:, :], top_full[:, :], ALU.add).then_inc(s_top, 1)
                dve.wait_ge(s_top, 3)
                dve.tensor_tensor(rest[:, :], top_walk[:, :], before_last[0:1, :], ALU.subtract).then_inc(s_top, 1)
                dve.wait_ge(s_top, 4)
                dve.tensor_copy(rest_number[:, :], rest[:, :]).then_inc(s_rest, 1)
                for k in range(SLOTS):
                    dve.tensor_scalar(slot_rest[:, k, :], rest[:, :], float(-k * CHUNK), 0.0, ALU.add, ALU.max) \
                        .then_inc(s_top, 1)
                dve.wait_ge(s_top, 4 + SLOTS)
                dve.tensor_scalar(rest_landed[:, :, :], slot_rest[:, :, :], float(CHUNK), float(2 * 16),
                                  ALU.min, ALU.mult).then_inc(s_rest, 1)

            def group(g, first, end, before, older):
                if older:
                    mlp_home(g - 2)
                    mlp_prelu1(g - 2)
                dve.wait_ge(s_target, (g + 1) * 16)
                dve.tensor_copy(q_cur[:, :], head[:, 1, :]).then_inc(s_q_cur, 1)
                dve.wait_ge(s_q_cur, g + 1)
                adds = [first_landed(dve, g, k) if before else LANDED for k in range(SLOTS)]
                fill_first(0, g, adds[0])
                if before:
                    prelu1(*before)
                    scores(*before)
                    weigh(*before)
                if older:
                    mlp_result(g - 2)
                prelu0(0, first)
                fill_first(1, g, adds[1])
                if before:
                    finish(g - 1, first)
                if older:
                    mlp_place(g - 2)
                dve.wait_ge(s_group, g + 1)
                dve.memset(score[0][:, CHUNK:CHUNK + 1], -HUGE).then_inc(s_state, 1)
                dve.memset(keys[0][:, CHUNK, E:P + 1], 0.0).then_inc(s_state, 1)
                dve.wait_ge(s_head_idx, (g + 1) * 16)
                dve.tensor_tensor(left[:, :], head_idx[:, LENGTH:LENGTH + 1],
                                  before_last[:, bass.ds(g, 1)], ALU.subtract) \
                    .then_inc(s_left_set, 1)
                dve.wait_ge(s_state, (g + 1) * 2)
                dve.wait_ge(s_left_set, g + 1)
                prelu1(0, first)
                scores(0, first)
                weigh(0, first)
                if before:
                    mlp_prelu0(g - 1)
                dve.wait_ge(s_head, (g + 1) * (16 * 2))
                dve.tensor_copy(feat[:, 0:3 * E], head[:, :, :].rearrange("p a b -> p (a b)")) \
                    .then_inc(s_head_used, 1)
                prelu0(1, first)
                if not before:
                    count_rest()
                with dve.Fori(first + 1, end) as i:
                    step(0, i, (1, i - 1))
                    step(1, i, (0, i))

            dve.wait_ge(s_planned, 1)
            group(0, 0, first_end(dve), None, False)
            dve.wait_ge(s_rest, 2)
            first, end = passes(dve, 1)
            group(1, first, end, (1, first - 1), False)
            with dve.Fori(2, GROUPS) as g:
                first, end = passes(dve, g)
                group(g, first, end, (1, first - 1), True)
            end = dve.value_load(first_pass[0:1, GROUPS:GROUPS + 1], min_val=2, max_val=GROUPS * PASSES)
            mlp_home(GROUPS - 2)
            mlp_prelu1(GROUPS - 2)
            prelu1(1, end - 1)
            scores(1, end - 1)
            mlp_result(GROUPS - 2)
            weigh(1, end - 1)
            mlp_place(GROUPS - 2)
            finish(GROUPS - 1, end)

            mlp_home(GROUPS - 1)
            mlp_prelu0(GROUPS - 1)
            mlp_prelu1(GROUPS - 1)
            mlp_result(GROUPS - 1)
            mlp_place(GROUPS - 1)


def kernel(**inputs):
    import numpy as np
    import concourse.bacc as bacc
    from concourse.bass_utils import run_bass_kernel_spmd as run

    x = {name: np.asarray(a) for name, a in inputs.items()}
    tags, artists = x["r_hist_tags"], x["r_hist_artists"]
    B, T = tags.shape
    hist = np.stack([tags.reshape(B, T // CHUNK, CHUNK), artists.reshape(B, T // CHUNK, CHUNK)], axis=2)
    own = np.stack([x["r_user_id"], x["r_target_tag"], x["r_target_artist"], x["r_seq_lengths"],
                    *np.divmod(np.arange(B, dtype=np.int32), B // P)] + [np.zeros(B, np.int32)] * (META - 6), axis=1)
    arrays = {
        "lengths": x["r_seq_lengths"],
        "rows": np.concatenate([hist.reshape(B, 2 * T), own], axis=1),
        "user_table": x["L0_rec_user_table"], "tag_table": x["L0_rec_tag_table"],
        "artist_table": x["L0_rec_artist_table"],
    }
    for net in ("att", "mlp"):
        for n in range(3):
            arrays[f"{net}_w{n}"] = x[f"L0_rec_{net}_w{n}"].T
            arrays[f"{net}_b{n}"] = x[f"L0_rec_{net}_b{n}"]
            arrays[f"{net}_b{n}"] = arrays[f"{net}_b{n}"][:, None] if net == "mlp" and n < 2 \
                else arrays[f"{net}_b{n}"][None, :]
            if n < 2:
                arrays[f"{net}_a{n}"] = x[f"L0_rec_{net}_a{n}"]
    nc = bacc.Bacc("TRN2", target_bir_lowering=False, num_devices=1)
    arrays = {name: np.ascontiguousarray(a) for name, a in arrays.items()}
    t = {name: nc.dram_tensor(name, a.shape, mybir.dt.from_np(a.dtype), kind="ExternalInput").ap()
         for name, a in arrays.items()}
    keys_dram = nc.dram_tensor("keys_dram", (B,), F32, kind="Internal").ap()
    sorted_rows = nc.dram_tensor("sorted_rows", arrays["rows"].shape, I32, kind="Internal").ap()
    out = nc.dram_tensor("out", (B, 1), F32, kind="ExternalOutput").ap()
    net = [t[f"{n}_{p}"] for n in ("att", "mlp") for p in ("w0", "b0", "a0", "w1", "b1", "a1", "w2", "b2")]
    program(nc, t["lengths"], t["rows"], t["user_table"], t["tag_table"], t["artist_table"], *net,
            keys_dram, sorted_rows, out)
    return run(nc, [arrays], core_ids=[0]).results[0]["out"].reshape(B)
```
